# Optimizing a Trainium2 kernel written in Bass

```python
import numpy as np
import jax
import jax.numpy as jnp

def _softmax(x, axis=-1):
    return jax.nn.softmax(x, axis=axis)

def _gelu(x):
    return jax.nn.gelu(x, approximate=True)

def _silu(x):
    return jax.nn.silu(x)

def _sigmoid(x):
    return jax.nn.sigmoid(x)

def _layernorm(x, axis=-1, eps=1e-05):
    m = jnp.mean(x, axis=axis, keepdims=True)
    v = jnp.var(x, axis=axis, keepdims=True)
    return (x - m) / jnp.sqrt(v + eps)

def _scatter_add(tgt, idx, src, axis=0):
    return tgt.at[idx].add(src)

def _segment_sum(src, seg, n):
    return jax.ops.segment_sum(src, seg, n)
kernel_name = 'mk_gnn_ffn_d2_gnn_r8_5cd007'

def setup_inputs(seed: int=0):
    np.random.seed(seed)
    _w = jnp.asarray

    def _rec_inputs():
        import jax
        import jax.numpy as jnp
        _gk = jax.random.key(seed)
        x = -7.329e-05 + 0.9999 * jax.random.normal(jax.random.fold_in(_gk, 1), (1250, 1024), jnp.float32)
        src = jax.random.randint(jax.random.fold_in(_gk, 2), (20000,), 0, 1250, jnp.int32)
        dst = jax.random.randint(jax.random.fold_in(_gk, 3), (20000,), 0, 1250, jnp.int32)
        _o = jnp.argsort(dst, stable=True)
        src = src[_o]
        dst = dst[_o]
        edge_weight = -0.000130211 + 0.031236 * jax.random.normal(jax.random.fold_in(_gk, 12), (20000,), jnp.float32)
        return (x, src, dst, edge_weight)
    x, src, dst, edge_weight = _rec_inputs()

    def _L0_gnn_setup():
        import jax, jax.numpy as jnp
        import numpy as np
        INDIM = 1024
        OUTDIM = 1024
        NNZ = 8192
        N = 6250
        key = jax.random.key(seed)
        k1, k2, k3, k4, k5 = jax.random.split(key, 5)
        x = jax.random.normal(k1, (N, INDIM), dtype=jnp.float32)
        stdv = np.sqrt(6.0 / (INDIM + OUTDIM))
        nnz_weight = jax.random.uniform(k2, (NNZ,), dtype=jnp.float32, minval=-stdv, maxval=stdv)
        bias = jax.random.normal(k3, (OUTDIM,), dtype=jnp.float32) * 0.02
        row = jax.random.randint(k4, (NNZ,), 0, OUTDIM, dtype=jnp.int64)
        col = jax.random.randint(k5, (NNZ,), 0, INDIM, dtype=jnp.int64)
        edge_index = jnp.stack([row, col])
        return {'x': x, 'nnz_weight': nnz_weight, 'bias': bias, 'edge_index': edge_index}
    _L0_gnn_all = _L0_gnn_setup()
    _L0_gnn_in = {k: v for k, v in _L0_gnn_all.items() if k in ('bias',)}
    del _L0_gnn_all

    def _L0_ffn_setup():
        import jax, jax.numpy as jnp
        import numpy as np
        DIM = 1024
        HIDDEN = 512
        E = 8
        B, S = (2, 512)
        key = jax.random.key(seed)
        ks = jax.random.split(key, 8)
        sd = 1.0 / np.sqrt(DIM)
        sh = 1.0 / np.sqrt(HIDDEN)
        return {'x': jax.random.normal(ks[0], (B, S, DIM), dtype=jnp.float32), 'router_w': jax.random.uniform(ks[1], (DIM, E), jnp.float32, -sd, sd), 'router_b': jax.random.uniform(ks[2], (E,), jnp.float32, -sd, sd), 'w1': jax.random.uniform(ks[3], (E, DIM, 2 * HIDDEN), jnp.float32, -sd, sd), 'b1': jax.random.uniform(ks[4], (E, 2 * HIDDEN), jnp.float32, -sd, sd), 'w2': jax.random.uniform(ks[5], (E, HIDDEN, DIM), jnp.float32, -sh, sh), 'b2': jax.random.uniform(ks[6], (E, DIM), jnp.float32, -sh, sh)}
    _L0_ffn_all = _L0_ffn_setup()
    _L0_ffn_in = {k: v for k, v in _L0_ffn_all.items() if k in ('router_w', 'router_b', 'w1', 'b1', 'w2', 'b2')}
    del _L0_ffn_all

    def _L1_gnn_setup():
        import jax, jax.numpy as jnp
        import numpy as np
        N = 2500
        E = 40000
        IN = 1024
        HID = 256
        H = 4
        D = HID // H
        OUT = 1024
        EPS = 1e-06
        NEG_SLOPE = 0.2
        key = jax.random.key(seed)
        ks = jax.random.split(key, 8)
        x = jax.random.normal(ks[0], (N, IN), dtype=jnp.float32)
        edge_index = jax.random.randint(ks[1], (2, E), 0, N, dtype=jnp.int64)
        s = 0.02
        return {'x': x, 'edge_index': edge_index, 'rms_w': jnp.ones((IN,), dtype=jnp.float32), 'W_down': jax.random.normal(ks[2], (IN, HID), dtype=jnp.float32) * s, 'Wl': jax.random.normal(ks[3], (HID, HID), dtype=jnp.float32) * s, 'Wr': jax.random.normal(ks[4], (HID, HID), dtype=jnp.float32) * s, 'att': jax.random.normal(ks[5], (H, D), dtype=jnp.float32) * s, 'W_up': jax.random.normal(ks[6], (HID, OUT), dtype=jnp.float32) * s}
    _L1_gnn_all = _L1_gnn_setup()
    _L1_gnn_in = {k: v for k, v in _L1_gnn_all.items() if k in ('rms_w', 'W_down', 'Wl', 'Wr', 'att', 'W_up')}
    del _L1_gnn_all

    def _L1_ffn_setup():
        import jax, jax.numpy as jnp
        import numpy as np
        BLOCK = 16
        _GRID = jnp.array([0.0, 0.5, 1.0, 1.5, 2.0, 3.0, 4.0, 6.0], dtype=jnp.float32)
        _MID = jnp.array([0.25, 0.75, 1.25, 1.75, 2.5, 3.5, 5.0], dtype=jnp.float32)

        def fp4_quant_dequant(x):
            shape = x.shape
            xb = x.reshape(shape[:-1] + (shape[-1] // BLOCK, BLOCK))
            scale = jnp.max(jnp.abs(xb), axis=-1, keepdims=True) / 6.0
            scale = jnp.maximum(scale, jnp.float32(1e-12))
            xn = xb / scale
            idx = jnp.searchsorted(_MID, jnp.abs(xn))
            q = _GRID[idx] * jnp.sign(xn) * scale
            return q.reshape(shape)

        def fp4_linear(x, w):
            xq = fp4_quant_dequant(x)
            wq = fp4_quant_dequant(w)
            return jnp.einsum('bsk,nk->bsn', xq, wq)
        key = jax.random.key(seed)
        k1, k2, k3, k4 = jax.random.split(key, 4)
        H, I = (1024, 352)
        x = jax.random.normal(k1, (4, 512, H), dtype=jnp.float32)
        w_gate = jax.random.normal(k2, (I, H), dtype=jnp.float32) * 0.02
        w_up = jax.random.normal(k3, (I, H), dtype=jnp.float32) * 0.02
        w_down = jax.random.normal(k4, (H, I), dtype=jnp.float32) * 0.02
        return {'x': x, 'w_gate': w_gate, 'w_up': w_up, 'w_down': w_down}
    _L1_ffn_all = _L1_ffn_setup()
    _L1_ffn_in = {k: v for k, v in _L1_ffn_all.items() if k in ('w_gate', 'w_up', 'w_down')}
    del _L1_ffn_all
    return {'x': x, 'src': src, 'dst': dst, 'edge_weight': edge_weight, 'L0_gnn_bias': _L0_gnn_in['bias'], 'L0_ffn_router_w': _L0_ffn_in['router_w'], 'L0_ffn_router_b': _L0_ffn_in['router_b'], 'L0_ffn_w1': _L0_ffn_in['w1'], 'L0_ffn_b1': _L0_ffn_in['b1'], 'L0_ffn_w2': _L0_ffn_in['w2'], 'L0_ffn_b2': _L0_ffn_in['b2'], 'L1_gnn_rms_w': _L1_gnn_in['rms_w'], 'L1_gnn_W_down': _L1_gnn_in['W_down'], 'L1_gnn_Wl': _L1_gnn_in['Wl'], 'L1_gnn_Wr': _L1_gnn_in['Wr'], 'L1_gnn_att': _L1_gnn_in['att'], 'L1_gnn_W_up': _L1_gnn_in['W_up'], 'L1_ffn_w_gate': _L1_ffn_in['w_gate'], 'L1_ffn_w_up': _L1_ffn_in['w_up'], 'L1_ffn_w_down': _L1_ffn_in['w_down']}

def reference(x, src, dst, edge_weight, L0_gnn_bias, L0_ffn_router_w, L0_ffn_router_b, L0_ffn_w1, L0_ffn_b1, L0_ffn_w2, L0_ffn_b2, L1_gnn_rms_w, L1_gnn_W_down, L1_gnn_Wl, L1_gnn_Wr, L1_gnn_att, L1_gnn_W_up, L1_ffn_w_gate, L1_ffn_w_up, L1_ffn_w_down):
    import jax
    import jax.numpy as jnp

    def _L0_gnn_ref(x, nnz_weight, bias, edge_index):
        import jax, jax.numpy as jnp
        import numpy as np
        INDIM = 1024
        OUTDIM = 1024
        NNZ = 8192
        N = 6250
        row, col = (edge_index[0], edge_index[1])
        W = jnp.zeros((OUTDIM, INDIM), dtype=nnz_weight.dtype).at[row, col].add(nnz_weight)
        return x @ W.T + bias

    def _L0_ffn_ref(x, router_w, router_b, w1, b1, w2, b2):
        import jax, jax.numpy as jnp
        import numpy as np
        DIM = 1024
        HIDDEN = 512
        E = 8
        B, S = (2, 512)
        logits = jnp.einsum('bsd,de->bse', x, router_w) + router_b
        probs = jax.nn.softmax(logits, axis=-1)
        top1 = jnp.argmax(probs, axis=-1)
        out = jnp.zeros_like(x)
        for i in range(E):
            h = jnp.einsum('bsd,df->bsf', x, w1[i]) + b1[i]
            a, g = jnp.split(h, 2, axis=-1)
            y = jnp.einsum('bsh,hd->bsd', a * jax.nn.sigmoid(g), w2[i]) + b2[i]
            out = out + jnp.where((top1 == i)[..., None], y, 0.0)
        return out

    def _L1_gnn_ref(x, edge_index, rms_w, W_down, Wl, Wr, att, W_up):
        import jax, jax.numpy as jnp
        import numpy as np
        N = 2500
        E = 40000
        IN = 1024
        HID = 256
        H = 4
        D = HID // H
        OUT = 1024
        EPS = 1e-06
        NEG_SLOPE = 0.2
        n = x.shape[0]
        ms = jnp.mean(jnp.square(x), axis=-1, keepdims=True)
        x = x * jax.lax.rsqrt(ms + EPS) * rms_w
        x = x @ W_down
        loop = jnp.arange(n, dtype=edge_index.dtype)
        src = jnp.concatenate([edge_index[0], loop])
        dst = jnp.concatenate([edge_index[1], loop])
        xl = (x @ Wl).reshape(n, H, D)
        xr = (x @ Wr).reshape(n, H, D)
        msg = xl[src] + xr[dst]
        act = jnp.where(msg > 0, msg, NEG_SLOPE * msg)
        e = jnp.einsum('ehd,hd->eh', act, att)
        m = jax.ops.segment_max(e, dst, num_segments=n)
        p = jnp.exp(e - m[dst])
        denom = jax.ops.segment_sum(p, dst, num_segments=n)
        alpha = p / (denom[dst] + 1e-16)
        out = jax.ops.segment_sum(alpha[..., None] * xl[src], dst, num_segments=n)
        out = out.reshape(n, HID)
        return out @ W_up

    def _L1_ffn_ref(x, w_gate, w_up, w_down):
        import jax, jax.numpy as jnp
        import numpy as np
        BLOCK = 16
        _GRID = jnp.array([0.0, 0.5, 1.0, 1.5, 2.0, 3.0, 4.0, 6.0], dtype=jnp.float32)
        _MID = jnp.array([0.25, 0.75, 1.25, 1.75, 2.5, 3.5, 5.0], dtype=jnp.float32)

        def fp4_quant_dequant(x):
            shape = x.shape
            xb = x.reshape(shape[:-1] + (shape[-1] // BLOCK, BLOCK))
            scale = jnp.max(jnp.abs(xb), axis=-1, keepdims=True) / 6.0
            scale = jnp.maximum(scale, jnp.float32(1e-12))
            xn = xb / scale
            idx = jnp.searchsorted(_MID, jnp.abs(xn))
            q = _GRID[idx] * jnp.sign(xn) * scale
            return q.reshape(shape)

        def fp4_linear(x, w):
            xq = fp4_quant_dequant(x)
            wq = fp4_quant_dequant(w)
            return jnp.einsum('bsk,nk->bsn', xq, wq)
        gate = fp4_linear(x, w_gate)
        y = fp4_linear(x, w_up)
        h = jax.nn.silu(gate) * y
        return fp4_linear(h, w_down)
    edge_index = jnp.stack([src, dst])
    x = x + _L0_gnn_ref(_layernorm(x, axis=-1), edge_weight, L0_gnn_bias, edge_index)
    x = x + _L0_ffn_ref(_layernorm(x, axis=-1)[None], L0_ffn_router_w, L0_ffn_router_b, L0_ffn_w1, L0_ffn_b1, L0_ffn_w2, L0_ffn_b2)[0]
    x = x + _L1_gnn_ref(_layernorm(x, axis=-1), edge_index, L1_gnn_rms_w, L1_gnn_W_down, L1_gnn_Wl, L1_gnn_Wr, L1_gnn_att, L1_gnn_W_up)
    x = x + _L1_ffn_ref(_layernorm(x, axis=-1)[None], L1_ffn_w_gate, L1_ffn_w_up, L1_ffn_w_down)[0]
    return x

_drawn_inputs = setup_inputs


def setup_inputs(seed=0):
    import zlib

    import numpy as np

    out = dict(_drawn_inputs(seed))
    spreads = {'L1_gnn_rms_w': (1.0, 0.6)}
    factors = {'L0_ffn_b1': 5.766,
     'L1_gnn_W_down': 2.75,
     'L1_gnn_Wl': 2.763,
     'L1_gnn_Wr': 8.0,
     'L1_gnn_att': 8.0,
     'L1_gnn_W_up': 2.784}
    for name, (base, spread) in spreads.items():
        noise = np.random.default_rng([zlib.crc32(name.encode()), seed]).standard_normal(out[name].shape)
        drawn = base * np.exp(spread * noise) if base else spread * noise
        out[name] = jnp.asarray(drawn.astype(out[name].dtype))
    for name, factor in factors.items():
        out[name] = (out[name] * factor).astype(out[name].dtype)
    return out
```

```python
from contextlib import ExitStack

import concourse.bass as bass
from concourse import mybir

F32 = mybir.dt.float32
F16 = mybir.dt.float16
BF16 = mybir.dt.bfloat16
I32 = mybir.dt.int32
ALU = mybir.AluOpType
ACT = mybir.ActivationFunctionType
AX = mybir.AxisListType

P = 128
N = 1250
D = 1024
E = 20000
KT = D // P
NT = -(-N // P)
LAST = N - (NT - 1) * P
HALF = 512
EP = 125
EJ = E // EP
SLOTS = 4
GROUP = SLOTS * P
NG = 50
NS = NG * SLOTS
XE = 8
HID = 512
XS = (N + XE * (P - 1)) // P
HD = 256
NH = 4
HW = HD // NH
HW1 = HW + 1
FF = 352
QB = 16
BIG = 1.0e30
assert (E + NT * (GROUP - 1)) // GROUP <= NG


class Shared:
    pass


def after(engine, sem, value):
    if not isinstance(value, int) or value > 0:
        engine.wait_ge(sem, value)


def spread(ap, axis, count):
    v = ap.unsqueeze(axis)
    shape = list(v.shape)
    shape[axis] = count
    return v.broadcast_to(shape)


class Link:

    def __init__(self, engine, sem):
        self.engine, self.sem, self.count = engine, sem, 0

    def __call__(self, instruction):
        self.count += 1
        instruction.then_inc(self.sem, 1)
        self.engine.wait_ge(self.sem, self.count)


def pools(nc, ctx):
    def sb(name, shape, dt=F32):
        return ctx.enter_context(nc.sbuf_tensor(name, shape, dt))

    def ps(name, shape, dt=F32):
        return ctx.enter_context(nc.psum_tensor(name, shape, dt))

    held = []

    def sem(name):
        held.append(nc.alloc_semaphore(name))
        return held[-1]

    def give_back():
        if held:
            nc.clear_and_free_semaphores(held)
            nc.all_engine_barrier()

    ctx.callback(give_back)
    return sb, ps, sem


def build_constants(nc, c, edge_rows, token_rows, x):
    with ExitStack() as ctx:
        sb, ps, sem = pools(nc, ctx)
        empty_edges = sb("empty_edges", [P, NS, 4])
        zeros = sb("zeros", [P, D])
        iotas = sem("iotas")
        step = sem("const_step")
        fills_ready = sem("fills_ready")
        tail_zeroed = sem("tail_zeroed")
        stored = sem("fills_stored")
        block = ctx.enter_context(nc.Block())

        @block.gpsimd
        def _(pool):
            nc.gpsimd.iota(c.iota[:], pattern=[[1, D]], base=0, channel_multiplier=0,
                           allow_small_or_imprecise_dtypes=True).then_inc(iotas, 1)
            nc.gpsimd.iota(c.part[:], pattern=[[1, 1]], base=0, channel_multiplier=1,
                           allow_small_or_imprecise_dtypes=True).then_inc(iotas, 1)

        @block.vector
        def _(dve):
            link = Link(dve, step)
            link(nc.vector.memset(empty_edges[:], 0.0))
            nc.vector.memset(empty_edges[:, :, 1:2], -1.0).then_inc(fills_ready, 1)
            nc.vector.memset(zeros[:], 0.0).then_inc(fills_ready, 1)
            nc.vector.memset(c.x[:, NT - 1, :], 0.0).then_inc(tail_zeroed, 1)
            nc.vector.memset(c.ones[:], 1.0)
            dve.wait_ge(iotas, 2)
            nc.vector.tensor_scalar(c.before[:], c.iota[:, 0:P], c.part[:, 0:1], None, ALU.is_gt)
            link(nc.vector.tensor_scalar(c.ident[:], c.iota[:, 0:P], c.part[:, 0:1], None, ALU.is_equal))
            nc.vector.tensor_scalar(c.big_ident[:], spread(c.ident[:], 1, NH), BIG, None, ALU.mult)
            nc.vector.tensor_copy(c.row_select[:], spread(c.ident[0:SLOTS * NH, 0:SLOTS * NH], 2, P))

        @block.sync
        def _(sp):
            for t in range(NT - 1):
                sp.dma_start(c.x[:, t, :], x[t * P:(t + 1) * P, :]).then_inc(stored, 16)
            sp.wait_ge(fills_ready, 2)
            sp.dma_start(edge_rows.rearrange("(p s) k -> p (s k)", p=P),
                         empty_edges[:].rearrange("p s k -> p (s k)")).then_inc(stored, 16)
            for s in range(XS):
                sp.dma_start(token_rows[s * P:(s + 1) * P, :], zeros[:]).then_inc(stored, 16)
            sp.wait_ge(tail_zeroed, 1)
            sp.dma_start(c.x[0:LAST, NT - 1, :], x[(NT - 1) * P:N, :]).then_inc(stored, 16)
            sp.wait_ge(stored, 16 * (NT + 1 + XS))


def count_positions(nc, dve, link, k, rows, member, width, shift, slots, owner):
    classes = member.shape[1]
    for b in range(classes):
        nc.vector.tensor_tensor_scan(k.so_far[0:rows, b, :], k.all_one[0:rows, 0:width], member[:, b, :],
                                     0.0, ALU.mult, ALU.add).then_inc(k.scanned, 1)
    dve.wait_ge(k.scanned, classes)
    nc.vector.tensor_copy(k.row_total[0:rows, :], k.so_far[0:rows, :, width - 1]).then_inc(k.rows_counted, 1)
    dve.wait_ge(k.totals_ready, 1)
    link(nc.vector.tensor_scalar(k.units_f[:], k.totals[:, classes:2 * classes], float((1 << shift) - 1), None, ALU.add))
    link(nc.vector.tensor_copy(k.units_i[:], k.units_f[:]))
    link(nc.vector.tensor_scalar(k.units_i[:], k.units_i[:], shift, None, ALU.arith_shift_right))
    link(nc.vector.tensor_copy(k.units_f[:], k.units_i[:]))
    link(nc.vector.tensor_tensor_scan(k.units_end[:], k.all_one[:, 0:classes], k.units_f[:], 0.0, ALU.mult, ALU.add))
    link(nc.vector.tensor_tensor(k.start[:], k.units_end[:], k.units_f[:], ALU.subtract))
    link(nc.vector.tensor_scalar(k.start[:], k.start[:], float(1 << shift), -1.0, ALU.mult, ALU.add))
    link(nc.vector.tensor_tensor(k.start[:], k.start[:], k.totals[:, 0:classes], ALU.add))
    link(nc.vector.tensor_tensor(k.so_far[0:rows], k.so_far[0:rows], spread(k.start[0:rows, :], 2, width), ALU.add))
    link(nc.vector.tensor_tensor(k.so_far[0:rows], k.so_far[0:rows], member, ALU.mult))
    link(nc.vector.tensor_reduce(k.position_f[:], k.so_far[0:rows].rearrange("p b j -> p j b"), AX.X, ALU.add))
    link(nc.vector.tensor_copy(k.position[:], k.position_f[:]))
    link(nc.vector.tensor_tensor(k.ended[:], spread(k.units_end[0:1, :], 1, slots),
                                 spread(k.unit_number[0:1, 0:slots], 2, classes), ALU.is_le))
    link(nc.vector.tensor_reduce(k.owner_f[:], k.ended[:], AX.X, ALU.add))
    link(nc.vector.tensor_scalar(k.owner_f[:], k.owner_f[:], float(classes - 1), None, ALU.min))
    nc.vector.tensor_copy(owner, k.owner_f[:]).then_inc(k.owner_ready, 1)
    dve.wait_ge(k.owner_ready, 1)


def sorting_memory(sb, ps, sem, c, name, rows, classes, width, slots):
    k = Shared()
    k.so_far = sb(name + "_so_far", [P, classes, width])
    k.all_one = sb(name + "_all_one", [P, max(width, classes)])
    k.row_total = sb(name + "_row_total", [P, classes])
    k.totals = ps(name + "_totals", [P, 2 * classes])
    k.units_f = sb(name + "_units_f", [P, classes])
    k.units_i = sb(name + "_units_i", [P, classes], I32)
    k.units_end = sb(name + "_units_end", [P, classes])
    k.start = sb(name + "_start", [P, classes])
    k.position_f = sb(name + "_position_f", [rows, width])
    k.position = sb(name + "_position", [rows, width], I32)
    k.ended = sb(name + "_ended", [1, slots, classes])
    k.owner_f = sb(name + "_owner_f", [1, slots])
    k.unit_number = c.unit_number
    k.scanned = sem(name + "_scanned")
    k.rows_counted = sem(name + "_rows_counted")
    k.totals_ready = sem(name + "_totals_ready")
    k.owner_ready = sem(name + "_owner_ready")
    return k


def count_totals(nc, pe, c, k, rows, classes):
    pe.wait_ge(k.rows_counted, 1)
    pe.matmul(k.totals[:, 0:classes], c.before[0:rows, :], k.row_total[0:rows, :], start=True, stop=True)
    pe.matmul(k.totals[:, classes:2 * classes], c.ones[0:rows, :], k.row_total[0:rows, :],
              start=True, stop=True).then_inc(k.totals_ready, 1)


def sort_edges(nc, c, src, dst, weight, edge_rows):
    with ExitStack() as ctx:
        sb, ps, sem = pools(nc, ctx)
        src_i = sb("src_i", [EP, EJ], I32)
        dst_i = sb("dst_i", [EP, EJ], I32)
        bucket_i = sb("bucket_i", [EP, EJ], I32)
        weight_in = sb("weight_in", [EP, EJ])
        bucket = sb("bucket", [EP, EJ])
        dst_f = sb("dst_f", [EP, EJ])
        member = sb("member", [EP, NT, EJ])
        row = sb("edge_row", [EP, EJ, 4])
        low = sb("low", [EP, EJ], I32)
        address = sb("address", [EP, EJ], I32)
        k = sorting_memory(sb, ps, sem, c, "edge", EP, NT, EJ, NG)
        loaded = sem("edges_loaded")
        step = sem("edge_step")
        number_ready = sem("unit_number_ready")
        sorted_rows = sem("sorted_rows")
        reloaded = sem("edges_reloaded")
        block = ctx.enter_context(nc.Block())

        @block.sync
        def _(sp):
            sp.dma_start(dst_i[:], dst.rearrange("(p j) -> p j", p=EP)).then_inc(loaded, 16)
            sp.dma_start(src_i[:], src.rearrange("(p j) -> p j", p=EP)).then_inc(loaded, 16)
            sp.dma_start(weight_in[:], weight.rearrange("(p j) -> p j", p=EP)).then_inc(loaded, 16)
            sp.wait_ge(sorted_rows, 16 * EJ)
            sp.dma_start(c.edges[:].rearrange("p s k -> p (s k)"),
                         edge_rows.rearrange("(p s) k -> p (s k)", p=P)).then_inc(reloaded, 16)
            sp.wait_ge(reloaded, 16)

        @block.tensor
        def _(pe):
            count_totals(nc, pe, c, k, EP, NT)

        @block.vector
        def _(dve):
            link = Link(dve, step)
            link(nc.vector.memset(k.all_one[:], 1.0))
            dve.wait_ge(loaded, 48)
            link(nc.vector.tensor_scalar(bucket_i[:], dst_i[:], 7, None, ALU.arith_shift_right))
            link(nc.vector.tensor_copy(bucket[:], bucket_i[:]))
            link(nc.vector.tensor_copy(dst_f[:], dst_i[:]))
            link(nc.vector.tensor_tensor(member[:], spread(bucket[:], 1, NT),
                                         spread(c.unit_number[0:EP, 0:NT], 2, EJ), ALU.is_equal))
            link(nc.vector.memset(row[:], 0.0))
            link(nc.vector.tensor_copy(row[:, :, 0], src_i[:]))
            link(nc.vector.tensor_copy(row[:, :, 2], weight_in[:]))
            link(nc.vector.scalar_tensor_tensor(row[:, :, 1], bucket[:], -float(P), dst_f[:], ALU.mult, ALU.add))
            count_positions(nc, dve, link, k, EP, member[:], EJ, 9, NG, c.group_tile[:])
            link(nc.vector.tensor_scalar(low[:], k.position[:], P - 1, None, ALU.bitwise_and))
            link(nc.vector.tensor_scalar(k.position[:], k.position[:], 7, None, ALU.arith_shift_right))
            nc.vector.scalar_tensor_tensor(address[:], low[:], float(NS), k.position[:],
                                           ALU.mult, ALU.add).then_inc(number_ready, 1)

        @block.gpsimd
        def _(pool):
            pool.wait_ge(number_ready, 1)
            for j in range(EJ):
                pool.indirect_dma_start(out=edge_rows, out_offset=bass.IndirectOffsetOnAxis(ap=address[:, j:j + 1], axis=0),
                                        in_=row[:, j, :], in_offset=None).then_inc(sorted_rows, 16)


def build_weights(nc, c, mix):
    PAIR = 2
    with ExitStack() as ctx:
        sb, ps, sem = pools(nc, ctx)
        part = sb("weight_part", [P, 3, NS])
        part_low = sb("weight_part_low", [P, NS], BF16)
        rest = sb("weight_rest", [P, NS])
        source = sb("source_one_hot", [P, PAIR, SLOTS, D], BF16)
        target = sb("target_weighted", [P, PAIR, SLOTS, 3, P], BF16)
        product = ps("mix_product", [P, PAIR, D])
        step = sem("part_step")
        cleared = sem("mix_cleared")
        one_hots = sem("one_hots")
        products = sem("products")
        added = sem("added")
        block = ctx.enter_context(nc.Block())

        @block.gpsimd
        def _(pool):
            nc.gpsimd.memset(mix[:], 0.0).then_inc(cleared, 1)

        @block.vector
        def _(dve):
            link = Link(dve, step)
            link(nc.vector.tensor_copy(c.source_i[:], c.edges[:, :, 0]))
            link(nc.vector.tensor_copy(rest[:], c.edges[:, :, 2]))
            for q in range(3):
                link(nc.vector.tensor_copy(part_low[:], rest[:]))
                link(nc.vector.tensor_copy(part[:, q, :], part_low[:]))
                link(nc.vector.tensor_tensor(rest[:], rest[:], part[:, q, :], ALU.subtract))
            dve.wait_ge(cleared, 1)

            def prepare(g, j):
                after(dve, products, g - 1)
                for k in range(SLOTS):
                    s = g * SLOTS + k
                    nc.vector.tensor_scalar(source[:, j, k, :], c.iota[:], c.edges[:, bass.ds(s, 1), 0], None, ALU.is_equal)
                    for q in range(3):
                        ins = nc.vector.tensor_scalar(target[:, j, k, q, :], c.iota[:, 0:P], c.edges[:, bass.ds(s, 1), 1],
                                                      part[:, q, bass.ds(s, 1)], ALU.is_equal, ALU.mult)
                ins.then_inc(one_hots, 1)

            def add(g, j):
                tile = dve.value_load(c.group_tile[0:1, bass.ds(g, 1)], min_val=0, max_val=NT - 1)
                dve.wait_ge(products, g + 1)
                after(dve, added, g)
                nc.vector.tensor_tensor(mix[:, bass.ds(tile, 1), :], mix[:, bass.ds(tile, 1), :],
                                        product[:, j:j + 1, :], ALU.add).then_inc(added, 1)

            prepare(0, 0)
            prepare(1, 1)
            add(0, 0)
            with dve.Fori(1, NG // PAIR) as i:
                for j in range(PAIR):
                    prepare(i * PAIR + j, j)
                    add(i * PAIR + j - 1, 1 - j)
            add(NG - 1, 1)

        @block.tensor
        def _(pe):
            def multiply(g, j):
                pe.wait_ge(one_hots, g + 1)
                after(pe, added, g - 1)
                for half in range(2):
                    cols = slice(half * HALF, (half + 1) * HALF)
                    for k in range(SLOTS):
                        for q in range(3):
                            ins = pe.matmul(product[:, j, cols], target[:, j, k, q, :], source[:, j, k, cols],
                                            start=(k == 0 and q == 0), stop=(k == SLOTS - 1 and q == 2))
                ins.then_inc(products, 1)

            multiply(0, 0)
            multiply(1, 1)
            with pe.Fori(1, NG // PAIR) as i:
                for j in range(PAIR):
                    multiply(i * PAIR + j, j)


def pipeline(engine, count, stages, unroll=2):
    high = max(offset for offset, _ in stages)
    low = min(offset for offset, _ in stages)
    begin = unroll - low
    rounds = max(0, (count - high - begin) // unroll)
    if rounds < 2:
        rounds = 0
    end = begin + rounds * unroll

    def single(steps):
        for g in steps:
            for offset, work in stages:
                if 0 <= g + offset < count:
                    work(g + offset, (g + offset) % unroll, (g + offset) // unroll)

    single(range(-high, begin))
    if rounds:
        with engine.Fori(0, rounds) as i:
            for u in range(unroll):
                for offset, work in stages:
                    item = begin + u + offset
                    work(i * unroll + item, item % unroll, i + item // unroll)
    single(range(end, count - low))


class Normaliser:

    def __init__(self, name, nc, c, sb, ps, sem, keep=None, second_eps=None):
        self.nc, self.c, self.keep, self.second_eps = nc, c, keep, second_eps
        self.stats = sb(name + "_stats", [P, 2, 2, 6])
        self.moments = sb(name + "_moments", [P, 2, 2])
        self.spread_eps = sb(name + "_variance_eps", [P, 2, 2])
        self.inverse = sb(name + "_inverse_deviation", [P, 2, 2])
        self.power = sb(name + "_minus_half", [P, 1])
        if second_eps is not None:
            self.once = sb(name + "_once", [P, 2, 2])
            self.second = sb(name + "_second_eps", [P, 1])
            self.second_step = sem(name + "_second_step")
        self.normal = None if keep is not None else sb(name + "_normal", [P, 2, D])
        self.turned_sb = sb(name + "_normal_turned", [P, 2, KT, P])
        self.turned_ps = ps(name + "_normal_turned_ps", [P, 2, KT // 2, P])
        self.power_ready = sem(name + "_minus_half_ready")
        self.stats_ready = sem(name + "_stats_ready")
        self.stats_awaited = sem(name + "_stats_awaited")
        self.moments_ready = sem(name + "_moments_ready")
        self.variance_ready = sem(name + "_variance_ready")
        self.inverse_ready = sem(name + "_inverse_ready")
        self.plain_ready = sem(name + "_plain_ready")
        self.normal_ready = sem(name + "_normal_ready")
        self.turned = sem(name + "_normal_turned")
        self.taken = sem(name + "_normal_taken")
        self.products = sem(name + "_tile_products")

    def tile(self, t, j):
        return self.keep[:, bass.ds(t, 1), :] if self.keep is not None else self.normal[:, j:j + 1, :]

    def vector(self, dve, t, j, quantised=None):
        nc, x = self.nc, self.c.x
        for half in range(2):
            nc.vector.bn_stats(self.stats[:, j, half, :], x[:, bass.ds(t, 1), half * HALF:(half + 1) * HALF]
                               ).then_inc(self.stats_ready, 1)
        dve.wait_ge(self.stats_ready, 2 * t + 2)
        dve.sem_inc(self.stats_awaited, 1)
        nc.vector.bn_aggr(self.moments[:, j, :], self.stats[:, j, :, :]).then_inc(self.moments_ready, 1)
        dve.wait_ge(self.moments_ready, t + 1)
        nc.vector.tensor_scalar(self.spread_eps[:, j, 0:1], self.moments[:, j, 1:2], 1e-5, None, ALU.add
                                ).then_inc(self.variance_ready, 1)
        dve.wait_ge(self.inverse_ready, t + 1)
        if self.keep is None:
            after(dve, self.turned, 2 * (t - 1))
        ready = self.normal_ready if quantised is None else self.plain_ready
        nc.vector.tensor_scalar(self.tile(t, j), x[:, bass.ds(t, 1), :], self.moments[:, j, 0:1],
                                self.inverse[:, j, 0:1], ALU.subtract, ALU.mult).then_inc(ready, 1)
        if quantised is not None:
            dve.wait_ge(self.plain_ready, t + 1)
            quantised.vector(dve, t, self.normal[:, j, :], self.normal[:, j, :])

    def gpsimd(self, pool, t, j):
        pool.wait_ge(self.variance_ready, t + 1)
        if self.second_eps is not None:
            tt = self.nc.gpsimd.tensor_tensor
            once, var = self.once[:, j, 0:1], self.moments[:, j, 1:2]
            twice = self.once[:, j, 1:2]
            link = Link(pool, self.second_step)
            link.count = t * 5
            link(tt(once, self.spread_eps[:, j, 0:1], self.power[:], ALU.pow))
            link(tt(twice, once, once, ALU.mult))
            link(tt(twice, twice, var, ALU.mult))
            link(tt(twice, twice, self.second[:], ALU.add))
            link(tt(twice, twice, self.power[:], ALU.pow))
            tt(self.inverse[:, j, 0:1], once, twice, ALU.mult).then_inc(self.inverse_ready, 1)
            return
        self.nc.gpsimd.tensor_tensor(self.inverse[:, j, 0:1], self.spread_eps[:, j, 0:1], self.power[:], ALU.pow
                                     ).then_inc(self.inverse_ready, 1)

    def tensor(self, pe, t, j):
        pe.wait_ge(self.normal_ready, t + 1)
        for half in range(2):
            after(pe, self.taken, 2 * t + half - 1)
            for k in range(KT // 2):
                b = half * (KT // 2) + k
                cols = slice(b * P, (b + 1) * P)
                source = self.keep[:, t, cols] if self.keep is not None else self.normal[:, j, cols]
                ins = pe.transpose(self.turned_ps[:, half, k, :], source, self.c.ident[:])
            ins.then_inc(self.turned, 1)

    def scalar(self, act, t, j):
        for half in range(2):
            act.wait_ge(self.turned, 2 * t + half + 1)
            if half == 0:
                after(act, self.products, t - 1)
            self.nc.scalar.copy(self.turned_sb[:, j, half * 4:half * 4 + 4, :], self.turned_ps[:, half, :, :]
                                ).then_inc(self.taken, 1)


def apply_mix(nc, c, mix, bias):
    with ExitStack() as ctx:
        sb, ps, sem = pools(nc, ctx)
        norm = Normaliser("mixing", nc, c, sb, ps, sem)
        bias_rows = sb("bias_rows", [P, D])
        product = ps("node_product", [P, 2, D])
        bias_loaded = sem("bias_loaded")
        biased = sem("biased")
        summed = sem("node_summed")
        block = ctx.enter_context(nc.Block())

        @block.sync
        def _(sp):
            sp.dma_start(bias_rows[:], bias.partition_broadcast(P)).then_inc(bias_loaded, 16)

        @block.gpsimd
        def _(pool):
            nc.gpsimd.memset(norm.power[:], -0.5).then_inc(norm.power_ready, 1)
            pool.wait_ge(norm.power_ready, 1)
            pool.wait_ge(bias_loaded, 16)

            def add_bias(t, j, r):
                pool.wait_ge(norm.normal_ready, t + 1)
                tile = c.x[:, bass.ds(t, 1), :]
                nc.gpsimd.tensor_tensor(tile, tile, spread(bias_rows[:], 1, 1), ALU.add).then_inc(biased, 1)

            pipeline(pool, NT, [(1, lambda t, j, r: norm.gpsimd(pool, t, j)), (0, add_bias)])

        @block.vector
        def _(dve):
            def add_product(t, j, r):
                dve.wait_ge(biased, t + 1)
                dve.wait_ge(norm.products, t + 1)
                tile = c.x[:, bass.ds(t, 1), :]
                nc.vector.tensor_tensor(tile, tile, product[:, j:j + 1, :], ALU.add).then_inc(summed, 1)

            pipeline(dve, NT, [(1, lambda t, j, r: norm.vector(dve, t, j)), (0, add_product)])

        @block.scalar
        def _(act):
            pipeline(act, NT, [(0, lambda t, j, r: norm.scalar(act, t, j))])

        @block.tensor
        def _(pe):
            def multiply(t, j, r):
                pe.wait_ge(norm.taken, 2 * t + 2)
                after(pe, summed, t - 1)
                for half in range(2):
                    cols = slice(half * HALF, (half + 1) * HALF)
                    for k in range(KT):
                        ins = pe.matmul(product[:, j, cols], norm.turned_sb[:, j, k, :], mix[:, k, cols],
                                        start=(k == 0), stop=(k == KT - 1))
                ins.then_inc(norm.products, 1)

            pipeline(pe, NT, [(1, lambda t, j, r: norm.tensor(pe, t, j)), (0, multiply)])


def route(nc, c, router_w, router_b, token_rows):
    STEPS = 5
    with ExitStack() as ctx:
        sb, ps, sem = pools(nc, ctx)
        normal = sb("all_normal", [P, NT, D])
        norm = Normaliser("routing", nc, c, sb, ps, sem, keep=normal)
        weight = sb("router_weight", [P, KT, XE])
        bias = sb("router_bias", [P, XE])
        order = sb("expert_order", [P, XE])
        valid = sb("valid", [P, 1])
        logit = sb("logit", [P, 2, XE])
        best = sb("best", [P, 2, 1])
        first = sb("first", [P, 2, XE])
        member = sb("token_member", [P, XE, NT])
        product = ps("logit_product", [P, 2, HALF])
        k = sorting_memory(sb, ps, sem, c, "token", P, XE, NT, XS)
        loaded = sem("router_loaded")
        chosen = sem("choice_step")
        step = sem("token_step")
        placed = sem("tokens_placed")
        sent = sem("tokens_sent")
        block = ctx.enter_context(nc.Block())

        @block.sync
        def _(sp):
            sp.dma_start(weight[:], router_w.rearrange("(k p) e -> p k e", p=P)).then_inc(loaded, 16)
            sp.dma_start(bias[:], router_b.partition_broadcast(P)).then_inc(loaded, 16)

        @block.gpsimd
        def _(pool):
            nc.gpsimd.memset(norm.power[:], -0.5).then_inc(norm.power_ready, 1)
            pool.wait_ge(norm.power_ready, 1)
            pipeline(pool, NT, [(0, lambda t, j, r: norm.gpsimd(pool, t, j))])
            pool.wait_ge(placed, 1)
            for t in range(NT):
                rows = P if t < NT - 1 else LAST
                pool.indirect_dma_start(out=token_rows, out_offset=bass.IndirectOffsetOnAxis(ap=c.token_place[0:rows, t:t + 1], axis=0),
                                        in_=normal[0:rows, t, :], in_offset=None).then_inc(sent, 16)
            pool.wait_ge(sent, 16 * NT)

        @block.scalar
        def _(act):
            pipeline(act, NT, [(0, lambda t, j, r: norm.scalar(act, t, j))])

        @block.tensor
        def _(pe):
            pe.wait_ge(loaded, 32)

            def multiply(t, j, r):
                pe.wait_ge(norm.taken, 2 * t + 2)
                after(pe, chosen, STEPS * (t - 1))
                for b in range(KT):
                    ins = pe.matmul(product[:, j, 0:XE], norm.turned_sb[:, j, b, :], weight[:, b, :],
                                    start=(b == 0), stop=(b == KT - 1))
                ins.then_inc(norm.products, 1)

            norm.tensor(pe, 0, 0)
            for t in range(NT):
                if t + 1 < NT:
                    norm.tensor(pe, t + 1, (t + 1) % 2)
                multiply(t, t % 2, t // 2)
            count_totals(nc, pe, c, k, P, XE)

        @block.vector
        def _(dve):
            link = Link(dve, step)
            link(nc.vector.memset(k.all_one[:], 1.0))
            link(nc.vector.tensor_scalar(order[:], c.iota[:, 0:XE], -1.0, float(XE), ALU.mult, ALU.add))
            link(nc.vector.tensor_scalar(valid[:], c.part[:], float(LAST), None, ALU.is_lt))
            dve.wait_ge(loaded, 32)

            def choose(t, j, r):
                pick = Link(dve, chosen)
                pick.count = t * STEPS
                dve.wait_ge(norm.products, t + 1)
                pick(nc.vector.tensor_tensor(logit[:, j, :], product[:, j, 0:XE], bias[:], ALU.add))
                pick(nc.vector.tensor_reduce(best[:, j, :], logit[:, j, :], AX.X, ALU.max))
                pick(nc.vector.scalar_tensor_tensor(first[:, j, :], logit[:, j, :], best[:, j, :], order[:], ALU.is_ge, ALU.mult))
                pick(nc.vector.tensor_reduce(best[:, j, :], first[:, j, :], AX.X, ALU.max))
                pick(nc.vector.tensor_scalar(member[:, :, bass.ds(t, 1)], spread(order[:], 2, 1), best[:, j, :], None, ALU.is_equal))

            pipeline(dve, NT, [(1, lambda t, j, r: norm.vector(dve, t, j)), (0, choose)])
            link(nc.vector.tensor_scalar(member[:, :, NT - 1], member[:, :, NT - 1], valid[:, 0:1], None, ALU.mult))
            count_positions(nc, dve, link, k, P, member[:], NT, 7, XS, c.slot_expert[:])
            nc.vector.tensor_copy(c.token_place[:], k.position[:]).then_inc(placed, 1)


def run_experts(nc, c, w1, b1, w2, b2, token_rows, expert_rows):
    HB = HID // P
    with ExitStack() as ctx:
        sb, ps, sem = pools(nc, ctx)
        weight1 = sb("expert_weight1", [P, 2, KT, 2 * HID])
        weight2 = sb("expert_weight2", [P, 2, HB, D])
        bias1 = sb("expert_bias1", [1, 2, 2 * HID])
        bias2 = sb("expert_bias2", [1, 2, D])
        token = sb("slot_token", [P, 2, D])
        token_turned = sb("token_turned", [P, 2, KT, P])
        gate = sb("expert_gate", [P, 2, HID])
        hidden = sb("expert_hidden", [P, 2, HID])
        hidden_turned = sb("hidden_turned", [P, 2, HB, P])
        result = sb("expert_result", [P, 2, D])
        turned_ps = ps("token_turned_ps", [P, KT // 2, P])
        hidden_ps = ps("hidden_ps", [P, 2, 2 * HID])
        hidden_turned_ps = ps("hidden_turned_ps", [P, HB, P])
        result_ps = ps("result_ps", [P, 2, HALF])
        token_loaded = [sem(f"token_loaded{j}") for j in range(2)]
        first_loaded = [sem(f"first_loaded{j}") for j in range(2)]
        second_loaded = [sem(f"second_loaded{j}") for j in range(2)]
        tokens_turned = sem("tokens_turned")
        tokens_taken = sem("tokens_taken")
        hiddens = sem("hiddens")
        gates = sem("gates")
        gated = sem("gated")
        hiddens_turned = sem("hiddens_turned")
        hiddens_taken = sem("hiddens_taken")
        results = sem("results")
        results_taken = sem("results_taken")
        results_stored = [sem(f"results_stored{j}") for j in range(2)]
        block = ctx.enter_context(nc.Block())

        @block.sync
        def _(sp):
            def load_first(s, j, r):
                expert = sp.value_load(c.slot_expert[0:1, bass.ds(s, 1)], min_val=0, max_val=XE - 1)
                after(sp, tokens_turned, 2 * (s - 1))
                sp.dma_start(token[:, j, :], token_rows[bass.ds(s * P, P), :]).then_inc(token_loaded[j], 16)
                after(sp, hiddens, s - 1)
                sp.dma_start(weight1[:, j, :, :], w1[bass.ds(expert, 1), :, :].rearrange("e (k p) f -> p (e k) f", p=P)
                             ).then_inc(first_loaded[j], 16)
                sp.dma_start(bias1[:, j, :], b1[bass.ds(expert, 1), :]).then_inc(first_loaded[j], 16)

            def load_second(s, j, r):
                expert = sp.value_load(c.slot_expert[0:1, bass.ds(s, 1)], min_val=0, max_val=XE - 1)
                after(sp, results, 2 * (s - 1))
                sp.dma_start(weight2[:, j, :, :], w2[bass.ds(expert, 1), :, :].rearrange("e (k p) f -> p (e k) f", p=P)
                             ).then_inc(second_loaded[j], 16)
                sp.dma_start(bias2[:, j, :], b2[bass.ds(expert, 1), :]).then_inc(second_loaded[j], 16)

            pipeline(sp, XS, [(1, load_first), (0, load_second)])

        @block.tensor
        def _(pe):
            def turn_token(s, j, r, half):
                if half == 0:
                    pe.wait_ge(token_loaded[j], r * 16 + 16)
                after(pe, tokens_taken, 2 * s + half)
                for k in range(KT // 2):
                    b = half * (KT // 2) + k
                    ins = pe.transpose(turned_ps[:, k, :], token[:, j, b * P:(b + 1) * P], c.ident[:])
                ins.then_inc(tokens_turned, 1)

            def first(s, j, r):
                pe.wait_ge(tokens_taken, 2 * s + 2)
                pe.wait_ge(first_loaded[j], r * 32 + 32)
                after(pe, gated, s - 1)
                for half in range(2):
                    cols = slice(half * HID, (half + 1) * HID)
                    pe.matmul(hidden_ps[:, j, cols], c.ones[0:1, :], bias1[:, j, cols], start=True, stop=False)
                    for k in range(KT):
                        ins = pe.matmul(hidden_ps[:, j, cols], token_turned[:, j, k, :], weight1[:, j, k, cols],
                                        start=False, stop=(k == KT - 1))
                ins.then_inc(hiddens, 1)

            def second(s, j, r):
                pe.wait_ge(gated, s + 1)
                after(pe, hiddens_taken, s)
                for k in range(HB):
                    ins = pe.transpose(hidden_turned_ps[:, k, :], hidden[:, j, k * P:(k + 1) * P], c.ident[:])
                ins.then_inc(hiddens_turned, 1)
                pe.wait_ge(second_loaded[j], r * 32 + 32)
                pe.wait_ge(hiddens_taken, s + 1)
                for half in range(2):
                    cols = slice(half * HALF, (half + 1) * HALF)
                    after(pe, results_taken, 2 * s + half - 1)
                    pe.matmul(result_ps[:, half, :], c.ones[0:1, :], bias2[:, j, cols], start=True, stop=False)
                    for k in range(HB):
                        ins = pe.matmul(result_ps[:, half, :], hidden_turned[:, j, k, :], weight2[:, j, k, cols],
                                        start=False, stop=(k == HB - 1))
                    ins.then_inc(results, 1)

            pipeline(pe, XS, [(2, lambda s, j, r: turn_token(s, j, r, 0)), (2, lambda s, j, r: turn_token(s, j, r, 1)),
                              (1, first), (0, second)])

        @block.scalar
        def _(act):
            def take_token(s, j, r):
                for half in range(2):
                    act.wait_ge(tokens_turned, 2 * s + half + 1)
                    after(act, hiddens, s - 1)
                    nc.scalar.copy(token_turned[:, j, half * 4:half * 4 + 4, :], turned_ps[:]).then_inc(tokens_taken, 1)

            def squash(s, j, r):
                act.wait_ge(hiddens, s + 1)
                after(act, gated, s - 1)
                nc.scalar.activation(gate[:, j, :], hidden_ps[:, j, HID:2 * HID], ACT.Sigmoid).then_inc(gates, 1)

            def take_result(s, j, r):
                after(act, results_stored[j], r * 16)
                for half in range(2):
                    act.wait_ge(results, 2 * s + half + 1)
                    nc.scalar.copy(result[:, j, half * HALF:(half + 1) * HALF], result_ps[:, half, :]).then_inc(results_taken, 1)
                act.wait_ge(results_taken, 2 * s + 2)
                act.dma_start(expert_rows[bass.ds(s * P, P), :], result[:, j, :]).then_inc(results_stored[j], 16)

            pipeline(act, XS, [(2, take_token), (1, squash), (0, take_result)])
            for j in range(2):
                act.wait_ge(results_stored[j], 16 * len(range(j, XS, 2)))

        @block.vector
        def _(dve):
            def multiply(s, j, r):
                dve.wait_ge(gates, s + 1)
                after(dve, hiddens_turned, s - 1)
                nc.vector.tensor_tensor(hidden[:, j, :], hidden_ps[:, j, 0:HID], gate[:, j, :], ALU.mult).then_inc(gated, 1)

            def take_hidden(s, j, r):
                dve.wait_ge(hiddens_turned, s + 1)
                after(dve, results, 2 * (s - 1))
                nc.vector.tensor_copy(hidden_turned[:, j, :, :], hidden_turned_ps[:]).then_inc(hiddens_taken, 1)

            pipeline(dve, XS, [(1, multiply), (0, take_hidden)])


def attention_inputs(nc, c, att, w_down, w_l, w_r, rms_w, expert_rows, left_rows, both, best, total):
    HB = HD // P
    with ExitStack() as ctx:
        sb, ps, sem = pools(nc, ctx)
        norm = Normaliser("projecting", nc, c, sb, ps, sem, second_eps=1e-6)
        down = sb("down_weight", [P, KT, HD])
        scale = sb("rms_weight", [P, KT])
        sides = sb("side_weights", [P, HB, 2 * HD])
        gathered = sb("expert_gathered", [P, 2, D])
        narrow = sb("narrow_turned", [P, 2, HB, P])
        score = sb("self_score", [P, 2, HD])
        narrow_ps = ps("narrow_ps", [P, 2, HB, HALF // 2])
        sides_ps = ps("sides_ps", [P, 2, HALF])
        loaded = sem("projection_loaded")
        scaled = sem("down_scaled")
        rows_here = [sem(f"expert_rows_here{j}") for j in range(2)]
        updated = sem("nodes_updated")
        update_awaited = sem("update_awaited")
        narrow_taken = sem("narrow_taken")
        sided = sem("sided")
        sides_taken = sem("sides_taken")
        stored = sem("left_rows_stored")
        scored = sem("self_scored")
        block = ctx.enter_context(nc.Block())

        @block.sync
        def _(sp):
            sp.dma_start(scale[:], rms_w.rearrange("(k p) -> p k", p=P), allow_slow_non_contiguous=True).then_inc(loaded, 16)
            sp.dma_start(down[:], w_down.rearrange("(k p) f -> p k f", p=P)).then_inc(loaded, 16)
            sp.dma_start(sides[:, :, 0:HD], w_l.rearrange("(k p) f -> p k f", p=P)).then_inc(loaded, 16)
            sp.dma_start(sides[:, :, HD:2 * HD], w_r.rearrange("(k p) f -> p k f", p=P)).then_inc(loaded, 16)
            sp.dma_start(c.att_rows[:], att.rearrange("h d -> (h d)").partition_broadcast(P)).then_inc(loaded, 16)
            for t in range(NT):
                sp.wait_ge(sides_taken, t + 1)
                sp.dma_start(left_rows[t * P:(t + 1) * P, :], both[:, t, 0:HD]).then_inc(stored, 16)
            sp.wait_ge(stored, 16 * NT)

        @block.gpsimd
        def _(pool):
            nc.gpsimd.memset(norm.power[:], -0.5).then_inc(norm.power_ready, 1)
            nc.gpsimd.memset(norm.second[:], norm.second_eps).then_inc(norm.power_ready, 1)
            pool.wait_ge(norm.power_ready, 2)
            for t in range(NT + 1):
                if t < NT:
                    after(pool, updated, t - 1)
                    pool.indirect_dma_start(out=gathered[:, t % 2, :], out_offset=None, in_=expert_rows,
                                            in_offset=bass.IndirectOffsetOnAxis(ap=c.token_place[:, t:t + 1], axis=0)
                                            ).then_inc(rows_here[t % 2], 16)
                if t >= 1:
                    norm.gpsimd(pool, t - 1, (t - 1) % 2)

        @block.vector
        def _(dve):
            dve.wait_ge(loaded, 80)
            for k in range(KT):
                ins = nc.vector.tensor_scalar(down[:, k, :], down[:, k, :], scale[:, k:k + 1], None, ALU.mult)
            ins.then_inc(scaled, 1)

            def update(t, j, r):
                dve.wait_ge(rows_here[j], r * 16 + 16)
                tile = c.x[:, bass.ds(t, 1), :]
                nc.vector.tensor_tensor(tile, tile, gathered[:, j:j + 1, :], ALU.add).then_inc(updated, 1)
                dve.wait_ge(updated, t + 1)
                dve.sem_inc(update_awaited, 1)
                norm.vector(dve, t, j)

            def take(t, j, r):
                dve.wait_ge(sided, t + 1)
                nc.vector.tensor_scalar(both[:, bass.ds(t, 1), :], sides_ps[:, j:j + 1, :], 1.0, None, ALU.mult).then_inc(sides_taken, 1)

            pipeline(dve, NT, [(1, update), (0, take)])
            link = Link(dve, scored)
            for t in range(NT):
                j = t % 2
                link(nc.vector.tensor_tensor(score[:, j, :], both[:, t, 0:HD], both[:, t, HD:2 * HD], ALU.add))
                link(nc.vector.scalar_tensor_tensor(score[:, j, :], score[:, j, :], 0.2, score[:, j, :], ALU.mult, ALU.max))
                link(nc.vector.tensor_tensor(score[:, j, :], score[:, j, :], c.att_rows[:], ALU.mult))
                link(nc.vector.tensor_reduce(best[:, t, :], score[:, j, :].rearrange("p (h d) -> p h d", h=NH), AX.X, ALU.add))
            nc.vector.tensor_copy(total[:, :, :, 0:HW], both[:, :, 0:HD].rearrange("p t (h d) -> p t h d", h=NH))
            nc.vector.memset(total[:, :, :, HW:HW1], 1.0)

        @block.scalar
        def _(act):
            def take_narrow(t, j, r):
                act.wait_ge(norm.products, t + 1)
                after(act, sided, t - 1)
                nc.scalar.copy(narrow[:, j, :, :], narrow_ps[:, j, :, 0:P]).then_inc(narrow_taken, 1)

            pipeline(act, NT, [(1, lambda t, j, r: norm.scalar(act, t, j)), (0, take_narrow)])

        @block.tensor
        def _(pe):
            pe.wait_ge(scaled, 1)

            def narrow_down(t, j, r):
                pe.wait_ge(norm.taken, 2 * t + 2)
                after(pe, narrow_taken, t - 1)
                for m in range(HB):
                    for k in range(KT):
                        ins = pe.matmul(narrow_ps[:, j, m, 0:P], down[:, k, m * P:(m + 1) * P], norm.turned_sb[:, j, k, :],
                                        start=(k == 0), stop=(k == KT - 1))
                ins.then_inc(norm.products, 1)

            def make_sides(t, j, r):
                pe.wait_ge(narrow_taken, t + 1)
                after(pe, sides_taken, t - 1)
                for m in range(HB):
                    ins = pe.matmul(sides_ps[:, j, :], narrow[:, j, m, :], sides[:, m, :], start=(m == 0), stop=(m == HB - 1))
                ins.then_inc(sided, 1)

            pipeline(pe, NT, [(1, lambda t, j, r: norm.tensor(pe, t, j)), (0, narrow_down), (0, make_sides)])


def attend(nc, c, left_rows, both, best, total):
    B = 3
    GH = SLOTS * NH
    with ExitStack() as ctx:
        sb, ps, sem = pools(nc, ctx)
        index = sb("gather_index", [P, B, SLOTS], I32)
        left = sb("left_of_edge", [P, B, SLOTS, HD])
        right = sb("right_of_tile", [P, B, HD])
        member = sb("edge_member", [P, B, SLOTS, P])
        outside = sb("edge_outside", [P, B, SLOTS, P], BF16)
        member_turned = sb("edge_member_turned", [P, B, SLOTS, P])
        act_in = sb("message", [P, B, SLOTS, HD])
        act_out = sb("weighted_message", [P, B, SLOTS, HD])
        score = sb("edge_score", [P, B, GH])
        score_rows = sb("edge_score_rows", [GH, B, P])
        group_best = sb("group_best", [P, B, NH])
        new_best = sb("new_best", [P, B, NH])
        fade = sb("fade", [P, B, NH])
        below = sb("score_below_best", [P, B, GH])
        weight = sb("edge_weight_exp", [P, B, GH])
        value = sb("edge_value", [P, B, SLOTS, NH, HW1])
        small_ps = ps("attend_small_ps", [P, HALF])
        turned_ps = ps("member_turned_ps", [P, SLOTS, P])
        right_ps = ps("right_ps", [P, SLOTS, HD])
        spread_ps = ps("score_spread_ps", [P, 2, NH, P])
        best_ps = ps("best_of_edge_ps", [P, HALF])
        sum_ps = ps("edge_sum_ps", [P, HALF])
        S = Shared()
        S.indexed = sem("at_indexed")
        S.left_used = sem("at_left_used")
        S.prepared = sem("at_prepared")
        S.turned = sem("at_turned")
        S.turned_taken = sem("at_turned_taken")
        S.righted = sem("at_righted")
        S.messages = sem("at_messages")
        S.leaky = sem("at_leaky")
        S.weighted_m = sem("at_weighted_m")
        S.scored = sem("at_scored")
        S.scores_turned = sem("at_scores_turned")
        S.scores_rows = sem("at_scores_rows")
        S.spread_done = sem("at_spread_done")
        S.maxed = sem("at_maxed")
        S.part_max = sem("at_part_max")
        S.best_new = sem("at_best_new")
        S.faded = sem("at_faded")
        S.fade_diff = sem("at_fade_diff")
        S.best_stored = sem("at_best_stored")
        S.best_edge = sem("at_best_edge")
        S.belows = sem("at_belows")
        S.exps = sem("at_exps")
        S.values = sem("at_values")
        S.sums = sem("at_sums")
        S.rescaled = sem("at_rescaled")
        S.added = sem("at_added")
        S.rights = sem("at_rights")
        here = [sem(f"left_here{j}") for j in range(B)]
        block = ctx.enter_context(nc.Block())

        @block.gpsimd
        def _(pool):
            def gather(g, j, r):
                after(pool, S.values, g - B + 1)
                nc.gpsimd.tensor_copy(index[:, j, :], c.source_i[:, bass.ds(g * SLOTS, SLOTS)]).then_inc(S.indexed, 1)
                pool.wait_ge(S.indexed, g + 1)
                pool.sem_inc(S.left_used, 1)
                for k in range(SLOTS):
                    pool.indirect_dma_start(out=left[:, j, k, :], out_offset=None, in_=left_rows,
                                            in_offset=bass.IndirectOffsetOnAxis(ap=index[:, j, k:k + 1], axis=0)
                                            ).then_inc(here[j], 16)

            pipeline(pool, NG, [(0, gather)], unroll=B)

        @block.vector
        def _(dve):
            def tile_of(g):
                return dve.value_load(c.group_tile[0:1, bass.ds(g, 1)], min_val=0, max_val=NT - 1)

            def prepare(g, j, r):
                after(dve, S.sums, g - B + 1)
                tile = tile_of(g)
                nc.vector.tensor_copy(right[:, j:j + 1, :], both[:, bass.ds(tile, 1), HD:2 * HD])
                for k in range(SLOTS):
                    target = c.edges[:, bass.ds(g * SLOTS + k, 1), 1]
                    nc.vector.tensor_scalar(member[:, j, k, :], c.iota[:, 0:P], target, None, ALU.is_equal)
                    ins = nc.vector.tensor_scalar(outside[:, j, k, :], c.iota[:, 0:P], target, -1.0, ALU.is_equal, ALU.add)
                ins.then_inc(S.prepared, 1)

            def message(g, j, r):
                dve.wait_ge(here[j], r * SLOTS * 16 + SLOTS * 16)
                dve.wait_ge(S.righted, g + 1)
                nc.vector.tensor_tensor(act_in[:, j, :, :], right_ps[:], left[:, j, :, :], ALU.add).then_inc(S.messages, 1)
                dve.wait_ge(S.messages, g + 1)
                nc.vector.scalar_tensor_tensor(act_out[:, j, :, :], act_in[:, j, :, :], 0.2, act_in[:, j, :, :],
                                               ALU.mult, ALU.max).then_inc(S.leaky, 1)
                dve.wait_ge(S.leaky, g + 1)
                nc.vector.tensor_tensor(act_in[:, j, :, :], act_out[:, j, :, :], spread(c.att_rows[:], 1, SLOTS), ALU.mult
                                        ).then_inc(S.weighted_m, 1)
                dve.wait_ge(S.weighted_m, g + 1)
                nc.vector.tensor_reduce(score[:, j, :], act_in[:, j, :, :].rearrange("p k (h d) -> p (k h) d", h=NH),
                                        AX.X, ALU.add).then_inc(S.scored, 1)

            def maximum(g, j, r):
                tile = tile_of(g)
                for half in range(2):
                    dve.wait_ge(S.spread_done, 2 * g + half + 1)
                    out = group_best if half == 0 else new_best
                    nc.vector.tensor_reduce(out[:, j, :], spread_ps[:].rearrange("p k h e -> p h k e"), AX.XY, ALU.max
                                            ).then_inc(S.maxed, 1)
                dve.wait_ge(S.maxed, 2 * g + 2)
                nc.vector.tensor_tensor(group_best[:, j, :], group_best[:, j, :], new_best[:, j, :], ALU.max).then_inc(S.part_max, 1)
                dve.wait_ge(S.part_max, g + 1)
                after(dve, S.best_stored, g)
                nc.vector.tensor_tensor(new_best[:, j:j + 1, :], group_best[:, j:j + 1, :], best[:, bass.ds(tile, 1), :],
                                        ALU.max).then_inc(S.best_new, 1)
                dve.wait_ge(S.best_new, g + 1)
                nc.vector.tensor_tensor(fade[:, j:j + 1, :], best[:, bass.ds(tile, 1), :], new_best[:, j:j + 1, :],
                                        ALU.subtract).then_inc(S.fade_diff, 1)
                dve.wait_ge(S.fade_diff, g + 1)
                nc.vector.tensor_scalar(best[:, bass.ds(tile, 1), :], new_best[:, j:j + 1, :], 1.0, None, ALU.mult).then_inc(S.best_stored, 1)

            def lower(g, j, r):
                dve.wait_ge(S.best_edge, g + 1)
                nc.vector.tensor_tensor(below[:, j, :], score[:, j, :], best_ps[:, 0:GH], ALU.subtract).then_inc(S.belows, 1)
                dve.wait_ge(S.belows, 2 * g + 1)
                nc.vector.tensor_scalar(below[:, j, :], below[:, j, :], 0.0, None, ALU.min).then_inc(S.belows, 1)

            def weigh(g, j, r):
                dve.wait_ge(S.exps, g + 1)
                w = weight[:, j, :].rearrange("p (k h) -> p k h", k=SLOTS)
                flat = value[:, j, :, :, :].rearrange("p k h d -> p (k h) d")
                nc.vector.tensor_copy(flat[:, :, HW:HW1], spread(weight[:, j, :], 2, 1))
                nc.vector.tensor_tensor(flat[:, :, 0:HW], left[:, j, :, :].rearrange("p k (h d) -> p (k h) d", h=NH),
                                        spread(weight[:, j, :], 2, HW), ALU.mult).then_inc(S.values, 1)

            def accumulate(g, j, r):
                tile = tile_of(g)
                dve.wait_ge(S.faded, g + 1)
                after(dve, S.added, g)
                mine = total[:, bass.ds(tile, 1), :, :].rearrange("p t h d -> p (t h) d")
                nc.vector.tensor_tensor(mine, mine, spread(fade[:, j, :], 2, HW1), ALU.mult).then_inc(S.rescaled, 1)
                dve.wait_ge(S.rescaled, g + 1)
                dve.wait_ge(S.sums, g + 1)
                nc.vector.tensor_tensor(mine, mine, sum_ps[:, 0:NH * HW1].rearrange("p (h d) -> p h d", h=NH), ALU.add
                                        ).then_inc(S.added, 1)

            pipeline(dve, NG, [(1, prepare), (0, message), (-1, maximum), (-1, lower), (-1, weigh), (-1, accumulate)], unroll=B)

        @block.scalar
        def _(act):
            def take_member(g, j, r):
                act.wait_ge(S.turned, g + 1)
                after(act, S.best_edge, g - B + 1)
                nc.scalar.copy(member_turned[:, j, :, :], turned_ps[:]).then_inc(S.turned_taken, 1)

            def take_rows(g, j, r):
                act.wait_ge(S.scores_turned, g + 1)
                nc.scalar.copy(score_rows[:, j, :], small_ps[0:GH, 0:P]).then_inc(S.scores_rows, 1)

            def exponentials(g, j, r):
                act.wait_ge(S.fade_diff, g + 1)
                nc.scalar.activation(fade[:, j, :], fade[:, j, :], ACT.Exp).then_inc(S.faded, 1)
                act.wait_ge(S.belows, 2 * g + 2)
                nc.scalar.activation(weight[:, j, :], below[:, j, :], ACT.Exp).then_inc(S.exps, 1)

            pipeline(act, NG, [(1, take_member), (0, take_rows), (-1, exponentials)], unroll=B)

        @block.tensor
        def _(pe):
            def turn_member(g, j, r):
                pe.wait_ge(S.prepared, g + 1)
                after(pe, S.turned_taken, g)
                for k in range(SLOTS):
                    ins = pe.transpose(turned_ps[:, k, :], member[:, j, k, :], c.ident[:])
                ins.then_inc(S.turned, 1)

            def bring_right(g, j, r):
                pe.wait_ge(S.turned_taken, g + 1)
                after(pe, S.messages, g)
                for k in range(SLOTS):
                    ins = pe.matmul(right_ps[:, k, :], member_turned[:, j, k, :], right[:, j, :], start=True, stop=True)
                ins.then_inc(S.righted, 1)

            def turn_scores(g, j, r):
                pe.wait_ge(S.scored, g + 1)
                after(pe, S.scores_rows, g)
                pe.transpose(small_ps[0:GH, 0:P], score[:, j, :], c.ident[:]).then_inc(S.scores_turned, 1)

            def spread_scores(g, j, r):
                pe.wait_ge(S.scores_rows, g + 1)
                for half in range(2):
                    after(pe, S.maxed, 2 * g + half)
                    for kk in range(2):
                        k = half * 2 + kk
                        pe.matmul(spread_ps[:, kk, :, :], outside[:, j, k, :], c.big_ident[:], start=True, stop=False)
                        for h in range(NH):
                            ins = pe.matmul(spread_ps[:, kk, h, :], c.row_select[:, k * NH + h, :], score_rows[:, j, :],
                                            start=False, stop=(h == NH - 1))
                    ins.then_inc(S.spread_done, 1)

            def bring_best(g, j, r):
                pe.wait_ge(S.best_new, g + 1)
                after(pe, S.belows, 2 * g)
                for k in range(SLOTS):
                    ins = pe.matmul(best_ps[:, k * NH:(k + 1) * NH], member_turned[:, j, k, :], new_best[:, j, :],
                                    start=True, stop=True)
                ins.then_inc(S.best_edge, 1)

            def sum_up(g, j, r):
                pe.wait_ge(S.values, g + 1)
                after(pe, S.added, g)
                for k in range(SLOTS):
                    ins = pe.matmul(sum_ps[:, 0:NH * HW1], member[:, j, k, :],
                                    value[:, j, k, :, :].rearrange("p h d -> p (h d)"), start=(k == 0), stop=(k == SLOTS - 1))
                ins.then_inc(S.sums, 1)

            pipeline(pe, NG, [(1, turn_member), (1, bring_right), (-1, spread_scores), (-1, bring_best), (0, turn_scores),
                              (-1, sum_up)], unroll=B)


def attention_output(nc, c, w_up, total):
    HB = HD // P
    with ExitStack() as ctx:
        sb, ps, sem = pools(nc, ctx)
        up = sb("up_weight", [P, HB, D])
        denominator = sb("denominator", [P, 2, NH])
        mean = sb("attention_mean", [P, 2, NH, HW])
        turned = sb("attention_turned", [P, 2, HB, P])
        turned_ps = ps("attention_turned_ps", [P, 2, HALF])
        product = ps("attention_product", [P, 2, D])
        loaded = sem("up_loaded")
        divided = sem("divide_step")
        means = sem("attention_means")
        turns = sem("attention_turns")
        taken = sem("attention_taken")
        products = sem("attention_products")
        summed = sem("attention_summed")
        block = ctx.enter_context(nc.Block())

        @block.sync
        def _(sp):
            sp.dma_start(up[:], w_up.rearrange("(k p) f -> p k f", p=P)).then_inc(loaded, 16)

        @block.vector
        def _(dve):
            def divide(t, j, r):
                link = Link(dve, divided)
                link.count = t * 2
                link(nc.vector.tensor_scalar(denominator[:, j, :], total[:, bass.ds(t, 1), :, HW], 1e-16, None, ALU.add))
                link(nc.vector.reciprocal(denominator[:, j, :], denominator[:, j, :]))
                after(dve, turns, t - 1)
                nc.vector.tensor_tensor(mean[:, j, :, :], total[:, bass.ds(t, 1), :, 0:HW].rearrange("p t h d -> p (t h) d"),
                                        spread(denominator[:, j, :], 2, HW), ALU.mult).then_inc(means, 1)

            def add_product(t, j, r):
                dve.wait_ge(products, t + 1)
                tile = c.x[:, bass.ds(t, 1), :]
                nc.vector.tensor_tensor(tile, tile, product[:, j:j + 1, :], ALU.add).then_inc(summed, 1)

            pipeline(dve, NT, [(1, divide), (0, add_product)])

        @block.scalar
        def _(act):
            def take(t, j, r):
                act.wait_ge(turns, t + 1)
                after(act, products, t - 1)
                nc.scalar.copy(turned[:, j, :, :], turned_ps[:, j, 0:HD].rearrange("p (m e) -> p m e", m=HB)).then_inc(taken, 1)

            pipeline(act, NT, [(0, take)])

        @block.tensor
        def _(pe):
            pe.wait_ge(loaded, 16)

            def turn(t, j, r):
                pe.wait_ge(means, t + 1)
                after(pe, taken, t - 1)
                flat = mean[:, j, :, :].rearrange("p h d -> p (h d)")
                for m in range(HB):
                    ins = pe.transpose(turned_ps[:, j, m * P:(m + 1) * P], flat[:, m * P:(m + 1) * P], c.ident[:])
                ins.then_inc(turns, 1)

            def multiply(t, j, r):
                pe.wait_ge(taken, t + 1)
                after(pe, summed, t - 1)
                for half in range(2):
                    cols = slice(half * HALF, (half + 1) * HALF)
                    for m in range(HB):
                        ins = pe.matmul(product[:, j, cols], turned[:, j, m, :], up[:, m, cols], start=(m == 0), stop=(m == HB - 1))
                ins.then_inc(products, 1)

            pipeline(pe, NT, [(1, turn), (0, multiply)])


class Quantiser:

    VECTOR = 14

    def __init__(self, name, nc, sb, sem, width):
        self.nc, self.width, self.blocks = nc, width, width // QB
        self.scale = sb(name + "_scale", [P, self.blocks])
        self.inverse = sb(name + "_inverse", [P, self.blocks])
        self.size = sb(name + "_size", [P, width])
        self.sign = sb(name + "_sign", [P, width])
        self.level = sb(name + "_level", [P, width])
        self.step = sem(name + "_step")
        self.signs = sem(name + "_signs")
        self.done = sem(name + "_done")

    def scalar(self, act, n, source, rows=P):
        after(act, self.done, n)
        self.nc.scalar.activation(self.sign[0:rows, :], source, ACT.Sign).then_inc(self.signs, 1)

    def vector(self, dve, n, source, target, rows=P):
        v = self.nc.vector
        blocks = lambda ap: ap.rearrange("p (b q) -> p b q", q=QB)
        scale, inverse = self.scale[0:rows, :], self.inverse[0:rows, :]
        size, level, sign = self.size[0:rows, :], self.level[0:rows, :], self.sign[0:rows, :]
        link = Link(dve, self.step)
        link.count = n * self.VECTOR
        after(dve, self.done, n)
        link(v.tensor_reduce(scale, blocks(source), AX.X, ALU.max, apply_absolute_value=True))
        link(v.tensor_scalar(scale, scale, 1.0 / 6.0, 1e-12, ALU.mult, ALU.max))
        link(v.reciprocal(inverse, scale))
        dve.wait_ge(self.signs, n + 1)
        link(v.tensor_tensor(size, source, sign, ALU.mult))
        link(v.tensor_tensor(blocks(size), blocks(size), spread(inverse, 2, QB), ALU.mult))
        link(v.tensor_scalar(level, size, 5.0, 2.0, ALU.is_gt, ALU.mult))
        link(v.scalar_tensor_tensor(level, size, 3.5, level, ALU.is_gt, ALU.add))
        link(v.scalar_tensor_tensor(level, size, 2.5, level, ALU.is_gt, ALU.add))
        link(v.tensor_scalar(level, level, 2.0, None, ALU.mult))
        for bound in (1.75, 1.25, 0.75, 0.25):
            link(v.scalar_tensor_tensor(level, size, bound, level, ALU.is_gt, ALU.add))
        link(v.scalar_tensor_tensor(level, level, 0.5, sign, ALU.mult, ALU.mult))
        v.tensor_tensor(blocks(target), blocks(level), spread(scale, 2, QB), ALU.mult).then_inc(self.done, 1)


def quantise_weights(nc, c, q_gate, q_up, q_down, in_turned, down_turned):
    FB = -(-FF // P)
    tiles = [(w, n, min(P, FF - n * P)) for w in range(2) for n in range(FB)]
    with ExitStack() as ctx:
        sb, ps, sem = pools(nc, ctx)
        raw = sb("raw_weight", [P, 2, D])
        raw_down = sb("raw_down", [P, 2, FF])
        level = sb("weight_level", [P, 2, D])
        level_down = sb("down_level", [P, 2, FF])
        wide = Quantiser("weight_quantiser", nc, sb, sem, D)
        thin = Quantiser("down_quantiser", nc, sb, sem, FF)
        turned_ps = ps("weight_turned_ps", [P, 2, 2, KT // 2, P])
        down_ps = ps("down_turned_ps", [P, 2, HALF])
        here = [sem(f"raw_weight_here{j}") for j in range(2)]
        down_here = [sem(f"raw_down_here{j}") for j in range(2)]
        turned = sem("weights_turned")
        taken = sem("weights_taken")
        down_done = sem("down_turned")
        down_taken = sem("down_taken")
        block = ctx.enter_context(nc.Block())

        def take(dve, n):
            w, b, rows = tiles[n]
            dve.wait_ge(turned, n + 1)
            first = w * FF + b * P
            nc.vector.tensor_copy(in_turned[:, :, first:first + rows],
                                  turned_ps[:, n % 2, :, :, 0:rows].rearrange("p h k r -> p (h k) r")).then_inc(taken, 1)

        def take_down(dve, n):
            dve.wait_ge(down_done, n + 1)
            for b in range(FB):
                rows = min(P, FF - b * P)
                ins = nc.vector.tensor_copy(down_turned[0:rows, b, n * P:(n + 1) * P], down_ps[0:rows, n % 2, b * P:(b + 1) * P])
            ins.then_inc(down_taken, 1)

        @block.sync
        def _(sp):
            for n, (w, b, rows) in enumerate(tiles):
                after(sp, wide.done, n - 1)
                sp.dma_start(raw[0:rows, n % 2, :], (q_gate, q_up)[w][b * P:b * P + rows, :]).then_inc(here[n % 2], 16)
            for n in range(KT):
                after(sp, thin.done, n - 1)
                sp.dma_start(raw_down[:, n % 2, :], q_down[n * P:(n + 1) * P, :]).then_inc(down_here[n % 2], 16)

        @block.scalar
        def _(act):
            for n, (w, b, rows) in enumerate(tiles):
                act.wait_ge(here[n % 2], 16 * (n // 2 + 1))
                wide.scalar(act, n, raw[0:rows, n % 2, :], rows)
            for n in range(KT):
                act.wait_ge(down_here[n % 2], 16 * (n // 2 + 1))
                thin.scalar(act, n, raw_down[:, n % 2, :])

        @block.vector
        def _(dve):
            for n, (w, b, rows) in enumerate(tiles):
                dve.wait_ge(here[n % 2], 16 * (n // 2 + 1))
                after(dve, turned, n - 1)
                wide.vector(dve, n, raw[0:rows, n % 2, :], level[0:rows, n % 2, :], rows)
                if n:
                    take(dve, n - 1)
            take(dve, len(tiles) - 1)
            for n in range(KT):
                dve.wait_ge(down_here[n % 2], 16 * (n // 2 + 1))
                after(dve, down_done, n - 1)
                thin.vector(dve, n, raw_down[:, n % 2, :], level_down[:, n % 2, :])
                if n:
                    take_down(dve, n - 1)
            take_down(dve, KT - 1)

        @block.tensor
        def _(pe):
            for n, (w, b, rows) in enumerate(tiles):
                pe.wait_ge(wide.done, n + 1)
                after(pe, taken, n - 1)
                for k in range(KT):
                    ins = pe.transpose(turned_ps[:, n % 2, k // 4, k % 4, 0:rows], level[0:rows, n % 2, k * P:(k + 1) * P],
                                       c.ident[0:rows, 0:rows])
                ins.then_inc(turned, 1)
            for n in range(KT):
                pe.wait_ge(thin.done, n + 1)
                after(pe, down_taken, n - 1)
                for b in range(FB):
                    cols = min(P, FF - b * P)
                    ins = pe.transpose(down_ps[0:cols, n % 2, b * P:(b + 1) * P], level_down[:, n % 2, b * P:b * P + cols], c.ident[:])
                ins.then_inc(down_done, 1)


def quantised_feed_forward(nc, c, q_gate, q_up, q_down, out):
    FB = -(-FF // P)
    with ExitStack() as ctx:
        sb, ps, sem = pools(nc, ctx)
        in_turned = sb("in_turned", [P, KT, 2 * FF])
        down_turned = sb("down_weight_turned", [P, FB, D])
        quantise_weights(nc, c, q_gate, q_up, q_down, in_turned, down_turned)
        norm = Normaliser("last", nc, c, sb, ps, sem)
        first = Quantiser("node_quantiser", nc, sb, sem, D)
        norm.normal_ready = first.done
        second = Quantiser("hidden_quantiser", nc, sb, sem, FF)
        gate = sb("last_gate", [P, 2, FF])
        hidden = sb("last_hidden", [P, 2, FF])
        level = sb("hidden_level", [P, 2, FF])
        hidden_turned = sb("last_hidden_turned", [P, 2, FB, P])
        gate_ps = ps("last_gate_ps", [P, HALF])
        up_ps = ps("last_up_ps", [P, HALF])
        hidden_ps = ps("last_hidden_ps", [P, HALF])
        result_ps = ps("last_result_ps", [P, 2, HALF])
        plain = sem("last_plain")
        gated = sem("last_gated")
        sized = sem("last_sized")
        hiddens = sem("last_hiddens")
        turns = sem("last_turns")
        taken = sem("last_hidden_taken")
        results = sem("last_results")
        summed = sem("last_summed")
        stored = sem("last_stored")
        block = ctx.enter_context(nc.Block())

        @block.gpsimd
        def _(pool):
            nc.gpsimd.memset(norm.power[:], -0.5).then_inc(norm.power_ready, 1)
            pool.wait_ge(norm.power_ready, 1)
            pipeline(pool, NT, [(0, lambda t, j, r: norm.gpsimd(pool, t, j))])

        @block.vector
        def _(dve):
            def normalise(t, j, r):
                norm.vector(dve, t, j, quantised=first)

            def make_hidden(t, j, r):
                dve.wait_ge(gated, t + 1)
                nc.vector.tensor_tensor(gate[:, j, :], gate[:, j, :], gate_ps[:, 0:FF], ALU.mult).then_inc(sized, 1)
                dve.wait_ge(sized, t + 1)
                nc.vector.tensor_tensor(hidden[:, j, :], gate[:, j, :], up_ps[:, 0:FF], ALU.mult).then_inc(hiddens, 1)
                dve.wait_ge(hiddens, t + 1)
                after(dve, turns, t - 1)
                second.vector(dve, t, hidden[:, j, :], level[:, j, :])

            def add_result(t, j, r):
                for half in range(2):
                    dve.wait_ge(results, 2 * t + half + 1)
                    tile = c.x[:, bass.ds(t, 1), half * HALF:(half + 1) * HALF]
                    nc.vector.tensor_tensor(tile, tile, result_ps[:, half:half + 1, :], ALU.add).then_inc(summed, 1)

            pipeline(dve, NT, [(1, normalise), (0, make_hidden), (0, add_result)])

        @block.scalar
        def _(act):
            def plain_sign(t, j, r):
                act.wait_ge(norm.plain_ready, t + 1)
                first.scalar(act, t, norm.normal[:, j, :])

            def squash(t, j, r):
                act.wait_ge(norm.products, t + 1)
                after(act, second.done, t - 1)
                nc.scalar.activation(gate[:, j, :], gate_ps[:, 0:FF], ACT.Sigmoid).then_inc(gated, 1)

            def hidden_sign(t, j, r):
                act.wait_ge(hiddens, t + 1)
                second.scalar(act, t, hidden[:, j, :])

            def take(t, j, r):
                act.wait_ge(turns, t + 1)
                after(act, results, 2 * (t - 1))
                for b in range(FB):
                    rows = min(P, FF - b * P)
                    ins = nc.scalar.copy(hidden_turned[0:rows, j, b, :], hidden_ps[0:rows, b * P:(b + 1) * P])
                ins.then_inc(taken, 1)

            pipeline(act, NT, [(1, plain_sign), (1, lambda t, j, r: norm.scalar(act, t, j)), (0, squash),
                               (0, hidden_sign), (0, take)])

        @block.tensor
        def _(pe):
            def multiply(t, j, r):
                pe.wait_ge(norm.taken, 2 * t + 2)
                after(pe, hiddens, t)
                for side, bank in ((0, gate_ps), (1, up_ps)):
                    for k in range(KT):
                        ins = pe.matmul(bank[:, 0:FF], norm.turned_sb[:, j, k, :], in_turned[:, k, side * FF:(side + 1) * FF],
                                        start=(k == 0), stop=(k == KT - 1))
                ins.then_inc(norm.products, 1)

            def turn_hidden(t, j, r):
                pe.wait_ge(second.done, t + 1)
                after(pe, taken, t)
                for b in range(FB):
                    cols = min(P, FF - b * P)
                    ins = pe.transpose(hidden_ps[0:cols, b * P:(b + 1) * P], level[:, j, b * P:b * P + cols], c.ident[:])
                ins.then_inc(turns, 1)

            def project(t, j, r):
                pe.wait_ge(taken, t + 1)
                for half in range(2):
                    after(pe, summed, 2 * (t - 1) + half + 1)
                    for b in range(FB):
                        rows = min(P, FF - b * P)
                        ins = pe.matmul(result_ps[:, half, :], hidden_turned[0:rows, j, b, :],
                                        down_turned[0:rows, b, half * HALF:(half + 1) * HALF], start=(b == 0), stop=(b == FB - 1))
                    ins.then_inc(results, 1)

            pipeline(pe, NT, [(1, lambda t, j, r: norm.tensor(pe, t, j)), (0, multiply), (0, turn_hidden), (0, project)])

        @block.sync
        def _(sp):
            for t in range(NT):
                rows = P if t < NT - 1 else LAST
                sp.wait_ge(summed, 2 * t + 2)
                sp.dma_start(out[t * P:t * P + rows, :], c.x[0:rows, t, :]).then_inc(stored, 16)
            sp.wait_ge(stored, 16 * NT)


def gnn_ffn_kernel(nc, x, src, dst, edge_weight, gnn_bias, router_w, router_b, w1, b1, w2, b2,
                   rms_w, w_down, w_l, w_r, att, w_up, q_gate, q_up, q_down, out):
    edge_rows = nc.dram_tensor("edge_rows", [P * NS, 4], F32, kind="Internal").ap()
    token_rows = nc.dram_tensor("token_rows", [XS * P, D], F32, kind="Internal").ap()
    expert_rows = nc.dram_tensor("expert_rows", [XS * P, D], F32, kind="Internal").ap()
    left_rows = nc.dram_tensor("left_rows", [NT * P, HD], F32, kind="Internal").ap()
    with ExitStack() as ctx:
        sb, ps, sem = pools(nc, ctx)
        c = Shared()
        c.x = sb("x_nodes", [P, NT, D])
        c.iota = sb("iota", [P, D], F16)
        c.part = sb("part", [P, 1])
        c.ones = sb("ones", [P, P])
        c.before = sb("before", [P, P])
        c.ident = sb("ident", [P, P])
        c.big_ident = sb("big_ident", [P, NH, P], BF16)
        c.row_select = sb("row_select", [SLOTS * NH, SLOTS * NH, P])
        c.edges = sb("edges", [P, NS, 4])
        c.source_i = sb("source_i", [P, NS], I32)
        c.group_tile = sb("group_tile", [1, NG], I32)
        c.token_place = sb("token_place", [P, NT], I32)
        c.slot_expert = sb("slot_expert", [1, XS], I32)
        c.unit_number = c.iota
        build_constants(nc, c, edge_rows, token_rows, x)
        sort_edges(nc, c, src, dst, edge_weight, edge_rows)
        with ExitStack() as inner:
            mix = pools(nc, inner)[0]("mix", [P, NT, D])
            build_weights(nc, c, mix)
            apply_mix(nc, c, mix, gnn_bias)
        route(nc, c, router_w, router_b, token_rows)
        run_experts(nc, c, w1, b1, w2, b2, token_rows, expert_rows)
        with ExitStack() as inner:
            sbi = pools(nc, inner)[0]
            both = sbi("left_right", [P, NT, 2 * HD])
            best = sbi("best_score", [P, NT, NH])
            total = sbi("weighted_total", [P, NT, NH, HW1])
            c.att_rows = sbi("att_rows", [P, HD])
            attention_inputs(nc, c, att, w_down, w_l, w_r, rms_w, expert_rows, left_rows, both, best, total)
            attend(nc, c, left_rows, both, best, total)
            attention_output(nc, c, w_up, total)
        quantised_feed_forward(nc, c, q_gate, q_up, q_down, out)


INPUTS = ["x", "src", "dst", "edge_weight", "L0_gnn_bias", "L0_ffn_router_w", "L0_ffn_router_b", "L0_ffn_w1",
          "L0_ffn_b1", "L0_ffn_w2", "L0_ffn_b2", "L1_gnn_rms_w", "L1_gnn_W_down", "L1_gnn_Wl", "L1_gnn_Wr",
          "L1_gnn_att", "L1_gnn_W_up", "L1_ffn_w_gate", "L1_ffn_w_up", "L1_ffn_w_down"]


def kernel(**inputs):
    import numpy as np
    import concourse.bacc as bacc
    from concourse.bass_utils import run_bass_kernel_spmd

    nc = bacc.Bacc("TRN2", target_bir_lowering=False, num_devices=1)
    arrays, args = {}, []
    for name in INPUTS:
        a = np.ascontiguousarray(inputs[name])
        arrays["in_" + name] = a
        args.append(nc.dram_tensor("in_" + name, a.shape, mybir.dt.from_np(a.dtype), kind="ExternalInput").ap())
    out = nc.dram_tensor("out", (N, D), F32, kind="ExternalOutput").ap()
    gnn_ffn_kernel(nc, *args, out)
    result = run_bass_kernel_spmd(nc, [arrays], core_ids=[0])
    return result.results[0]["out"]
```

```python
from contextlib import ExitStack

import concourse.bass as bass
from concourse import mybir

F32 = mybir.dt.float32
F16 = mybir.dt.float16
BF16 = mybir.dt.bfloat16
I32 = mybir.dt.int32
ALU = mybir.AluOpType
ACT = mybir.ActivationFunctionType
AX = mybir.AxisListType

P = 128
N = 1250
D = 1024
E = 20000
KT = D // P
NT = -(-N // P)
LAST = N - (NT - 1) * P
HALF = 512
EP = 125
EJ = E // EP
SLOTS = 4
GROUP = SLOTS * P
NG = 50
NS = NG * SLOTS
XE = 8
HID = 512
XS = (N + XE * (P - 1)) // P
HD = 256
NH = 4
HW = HD // NH
GH = SLOTS * NH
HW1 = HW + 1
FF = 352
QB = 16
BIG = 1.0e30
assert (E + NT * (GROUP - 1)) // GROUP <= NG


class Shared:
    pass


def after(engine, sem, value):
    if not isinstance(value, int) or value > 0:
        engine.wait_ge(sem, value)


def spread(ap, axis, count):
    v = ap.unsqueeze(axis)
    shape = list(v.shape)
    shape[axis] = count
    return v.broadcast_to(shape)


class Link:

    def __init__(self, engine, sem):
        self.engine, self.sem, self.count = engine, sem, 0

    def __call__(self, instruction):
        self.count += 1
        instruction.then_inc(self.sem, 1)
        self.engine.wait_ge(self.sem, self.count)


def pools(nc, ctx):
    def sb(name, shape, dt=F32):
        return ctx.enter_context(nc.sbuf_tensor(name, shape, dt))

    def ps(name, shape, dt=F32):
        return ctx.enter_context(nc.psum_tensor(name, shape, dt))

    held = []

    def sem(name):
        held.append(nc.alloc_semaphore(name))
        return held[-1]

    def give_back():
        if held:
            nc.clear_and_free_semaphores(held)
            nc.all_engine_barrier()

    ctx.callback(give_back)
    return sb, ps, sem


def build_constants(nc, c, edge_rows, token_rows, x):
    with ExitStack() as ctx:
        sb, ps, sem = pools(nc, ctx)
        empty_edges = sb("empty_edges", [P, NS, 4])
        zeros = sb("zeros", [P, D])
        row_number_i = sb("row_number_i", [3 * GH, 1], I32)
        row_number = sb("row_number", [3 * GH, 1])
        iotas = sem("iotas")
        step = sem("const_step")
        fills_ready = sem("fills_ready")
        tail_zeroed = sem("tail_zeroed")
        stored = sem("fills_stored")
        block = ctx.enter_context(nc.Block())

        @block.gpsimd
        def _(pool):
            nc.gpsimd.iota(c.iota[:], pattern=[[1, D]], base=0, channel_multiplier=0,
                           allow_small_or_imprecise_dtypes=True).then_inc(iotas, 1)
            nc.gpsimd.iota(c.part[:], pattern=[[1, 1]], base=0, channel_multiplier=1,
                           allow_small_or_imprecise_dtypes=True).then_inc(iotas, 1)

        @block.vector
        def _(dve):
            link = Link(dve, step)
            link(nc.vector.memset(empty_edges[:], 0.0))
            nc.vector.memset(empty_edges[:, :, 1:2], -1.0).then_inc(fills_ready, 1)
            nc.vector.memset(zeros[:], 0.0).then_inc(fills_ready, 1)
            nc.vector.memset(c.x[:, NT - 1, :], 0.0).then_inc(tail_zeroed, 1)
            nc.vector.memset(c.ones[:], 1.0)
            dve.wait_ge(iotas, 2)
            nc.vector.tensor_scalar(c.before[:], c.iota[:, 0:P], c.part[:, 0:1], None, ALU.is_gt)
            link(nc.vector.tensor_scalar(c.ident[:], c.iota[:, 0:P], c.part[:, 0:1], None, ALU.is_equal))
            nc.vector.tensor_scalar(c.big_ident[:], spread(c.ident[:], 1, NH), BIG, None, ALU.mult)
            nc.vector.tensor_copy(c.ident_b[:], c.ident[:])
            link(nc.vector.tensor_copy(row_number_i[:], c.part[0:3 * GH, :]))
            link(nc.vector.tensor_scalar(row_number_i[:], row_number_i[:], GH - 1, None, ALU.bitwise_and))
            link(nc.vector.tensor_copy(row_number[:], row_number_i[:]))
            nc.vector.tensor_scalar(c.row_select[:], spread(c.iota[0:3 * GH, 0:GH], 2, P), row_number[:, 0:1], None, ALU.is_equal)

        @block.sync
        def _(sp):
            for t in range(NT - 1):
                sp.dma_start(c.x[:, t, :], x[t * P:(t + 1) * P, :]).then_inc(stored, 16)
            sp.wait_ge(fills_ready, 2)
            sp.dma_start(edge_rows.rearrange("(p s) k -> p (s k)", p=P),
                         empty_edges[:].rearrange("p s k -> p (s k)")).then_inc(stored, 16)
            for s in range(XS):
                sp.dma_start(token_rows[s * P:(s + 1) * P, :], zeros[:]).then_inc(stored, 16)
            sp.wait_ge(tail_zeroed, 1)
            sp.dma_start(c.x[0:LAST, NT - 1, :], x[(NT - 1) * P:N, :]).then_inc(stored, 16)
            sp.wait_ge(stored, 16 * (NT + 1 + XS))


def count_positions(nc, dve, link, k, rows, member, width, shift, slots, owner):
    classes = member.shape[1]
    for b in range(classes):
        nc.vector.tensor_tensor_scan(k.so_far[0:rows, b, :], k.all_one[0:rows, 0:width], member[:, b, :],
                                     0.0, ALU.mult, ALU.add).then_inc(k.scanned, 1)
    dve.wait_ge(k.scanned, classes)
    nc.vector.tensor_copy(k.row_total[0:rows, :], k.so_far[0:rows, :, width - 1]).then_inc(k.rows_counted, 1)
    dve.wait_ge(k.totals_ready, 1)
    link(nc.vector.tensor_scalar(k.units_f[:], k.totals[:, classes:2 * classes], float((1 << shift) - 1), None, ALU.add))
    link(nc.vector.tensor_copy(k.units_i[:], k.units_f[:]))
    link(nc.vector.tensor_scalar(k.units_i[:], k.units_i[:], shift, None, ALU.arith_shift_right))
    link(nc.vector.tensor_copy(k.units_f[:], k.units_i[:]))
    link(nc.vector.tensor_tensor_scan(k.units_end[:], k.all_one[:, 0:classes], k.units_f[:], 0.0, ALU.mult, ALU.add))
    link(nc.vector.tensor_tensor(k.start[:], k.units_end[:], k.units_f[:], ALU.subtract))
    link(nc.vector.tensor_scalar(k.start[:], k.start[:], float(1 << shift), -1.0, ALU.mult, ALU.add))
    link(nc.vector.tensor_tensor(k.start[:], k.start[:], k.totals[:, 0:classes], ALU.add))
    link(nc.vector.tensor_tensor(k.so_far[0:rows], k.so_far[0:rows], spread(k.start[0:rows, :], 2, width), ALU.add))
    link(nc.vector.tensor_tensor(k.so_far[0:rows], k.so_far[0:rows], member, ALU.mult))
    link(nc.vector.tensor_reduce(k.position_f[:], k.so_far[0:rows].rearrange("p b j -> p j b"), AX.X, ALU.add))
    link(nc.vector.tensor_copy(k.position[:], k.position_f[:]))
    link(nc.vector.tensor_tensor(k.ended[:], spread(k.units_end[0:1, :], 1, slots),
                                 spread(k.unit_number[0:1, 0:slots], 2, classes), ALU.is_le))
    link(nc.vector.tensor_reduce(k.owner_f[:], k.ended[:], AX.X, ALU.add))
    link(nc.vector.tensor_scalar(k.owner_f[:], k.owner_f[:], float(classes - 1), None, ALU.min))
    nc.vector.tensor_copy(owner, k.owner_f[:]).then_inc(k.owner_ready, 1)
    dve.wait_ge(k.owner_ready, 1)


def sorting_memory(sb, ps, sem, c, name, rows, classes, width, slots):
    k = Shared()
    k.so_far = sb(name + "_so_far", [P, classes, width])
    k.all_one = sb(name + "_all_one", [P, max(width, classes)])
    k.row_total = sb(name + "_row_total", [P, classes])
    k.totals = ps(name + "_totals", [P, 2 * classes])
    k.units_f = sb(name + "_units_f", [P, classes])
    k.units_i = sb(name + "_units_i", [P, classes], I32)
    k.units_end = sb(name + "_units_end", [P, classes])
    k.start = sb(name + "_start", [P, classes])
    k.position_f = sb(name + "_position_f", [rows, width])
    k.position = sb(name + "_position", [rows, width], I32)
    k.ended = sb(name + "_ended", [1, slots, classes])
    k.owner_f = sb(name + "_owner_f", [1, slots])
    k.unit_number = c.unit_number
    k.scanned = sem(name + "_scanned")
    k.rows_counted = sem(name + "_rows_counted")
    k.totals_ready = sem(name + "_totals_ready")
    k.owner_ready = sem(name + "_owner_ready")
    return k


def count_totals(nc, pe, c, k, rows, classes):
    pe.wait_ge(k.rows_counted, 1)
    pe.matmul(k.totals[:, 0:classes], c.before[0:rows, :], k.row_total[0:rows, :], start=True, stop=True)
    pe.matmul(k.totals[:, classes:2 * classes], c.ones[0:rows, :], k.row_total[0:rows, :],
              start=True, stop=True).then_inc(k.totals_ready, 1)


def sort_edges(nc, c, src, dst, weight, edge_rows):
    with ExitStack() as ctx:
        sb, ps, sem = pools(nc, ctx)
        src_i = sb("src_i", [EP, EJ], I32)
        dst_i = sb("dst_i", [EP, EJ], I32)
        bucket_i = sb("bucket_i", [EP, EJ], I32)
        weight_in = sb("weight_in", [EP, EJ])
        bucket = sb("bucket", [EP, EJ])
        dst_f = sb("dst_f", [EP, EJ])
        member = sb("member", [EP, NT, EJ])
        row = sb("edge_row", [EP, EJ, 4])
        low = sb("low", [EP, EJ], I32)
        address = sb("address", [EP, EJ], I32)
        k = sorting_memory(sb, ps, sem, c, "edge", EP, NT, EJ, NG)
        loaded = sem("edges_loaded")
        step = sem("edge_step")
        number_ready = sem("unit_number_ready")
        sorted_rows = sem("sorted_rows")
        reloaded = sem("edges_reloaded")
        block = ctx.enter_context(nc.Block())

        @block.sync
        def _(sp):
            sp.dma_start(dst_i[:], dst.rearrange("(p j) -> p j", p=EP)).then_inc(loaded, 16)
            sp.dma_start(src_i[:], src.rearrange("(p j) -> p j", p=EP)).then_inc(loaded, 16)
            sp.dma_start(weight_in[:], weight.rearrange("(p j) -> p j", p=EP)).then_inc(loaded, 16)
            sp.wait_ge(sorted_rows, 16 * EJ)
            sp.dma_start(c.edges[:].rearrange("p s k -> p (s k)"),
                         edge_rows.rearrange("(p s) k -> p (s k)", p=P)).then_inc(reloaded, 16)
            sp.wait_ge(reloaded, 16)

        @block.tensor
        def _(pe):
            count_totals(nc, pe, c, k, EP, NT)

        @block.vector
        def _(dve):
            link = Link(dve, step)
            link(nc.vector.memset(k.all_one[:], 1.0))
            dve.wait_ge(loaded, 48)
            link(nc.vector.tensor_scalar(bucket_i[:], dst_i[:], 7, None, ALU.arith_shift_right))
            link(nc.vector.tensor_copy(bucket[:], bucket_i[:]))
            link(nc.vector.tensor_copy(dst_f[:], dst_i[:]))
            link(nc.vector.tensor_tensor(member[:], spread(bucket[:], 1, NT),
                                         spread(c.unit_number[0:EP, 0:NT], 2, EJ), ALU.is_equal))
            link(nc.vector.memset(row[:], 0.0))
            link(nc.vector.tensor_copy(row[:, :, 0], src_i[:]))
            link(nc.vector.tensor_copy(row[:, :, 2], weight_in[:]))
            link(nc.vector.scalar_tensor_tensor(row[:, :, 1], bucket[:], -float(P), dst_f[:], ALU.mult, ALU.add))
            count_positions(nc, dve, link, k, EP, member[:], EJ, 9, NG, c.group_tile[:])
            link(nc.vector.tensor_scalar(low[:], k.position[:], P - 1, None, ALU.bitwise_and))
            link(nc.vector.tensor_scalar(k.position[:], k.position[:], 7, None, ALU.arith_shift_right))
            nc.vector.scalar_tensor_tensor(address[:], low[:], float(NS), k.position[:],
                                           ALU.mult, ALU.add).then_inc(number_ready, 1)

        @block.gpsimd
        def _(pool):
            pool.wait_ge(number_ready, 1)
            for j in range(EJ):
                pool.indirect_dma_start(out=edge_rows, out_offset=bass.IndirectOffsetOnAxis(ap=address[:, j:j + 1], axis=0),
                                        in_=row[:, j, :], in_offset=None).then_inc(sorted_rows, 16)


def build_weights(nc, c, mix):
    PAIR = 2
    with ExitStack() as ctx:
        sb, ps, sem = pools(nc, ctx)
        part = sb("weight_part", [P, 3, NS])
        part_low = sb("weight_part_low", [P, NS], BF16)
        rest = sb("weight_rest", [P, NS])
        source = sb("source_one_hot", [P, PAIR, SLOTS, D], BF16)
        target = sb("target_weighted", [P, PAIR, SLOTS, 3, P], BF16)
        product = ps("mix_product", [P, PAIR, D])
        step = sem("part_step")
        cleared = sem("mix_cleared")
        one_hots = sem("one_hots")
        products = sem("products")
        added = sem("added")
        block = ctx.enter_context(nc.Block())

        @block.gpsimd
        def _(pool):
            nc.gpsimd.memset(mix[:], 0.0).then_inc(cleared, 1)

        @block.vector
        def _(dve):
            link = Link(dve, step)
            link(nc.vector.tensor_copy(c.source_i[:], c.edges[:, :, 0]))
            link(nc.vector.tensor_copy(rest[:], c.edges[:, :, 2]))
            for q in range(3):
                link(nc.vector.tensor_copy(part_low[:], rest[:]))
                link(nc.vector.tensor_copy(part[:, q, :], part_low[:]))
                link(nc.vector.tensor_tensor(rest[:], rest[:], part[:, q, :], ALU.subtract))
            dve.wait_ge(cleared, 1)

            def prepare(g, j):
                after(dve, products, g - 1)
                for k in range(SLOTS):
                    s = g * SLOTS + k
                    nc.vector.tensor_scalar(source[:, j, k, :], c.iota[:], c.edges[:, bass.ds(s, 1), 0], None, ALU.is_equal)
                    for q in range(3):
                        ins = nc.vector.tensor_scalar(target[:, j, k, q, :], c.iota[:, 0:P], c.edges[:, bass.ds(s, 1), 1],
                                                      part[:, q, bass.ds(s, 1)], ALU.is_equal, ALU.mult)
                ins.then_inc(one_hots, 1)

            def add(g, j):
                tile = dve.value_load(c.group_tile[0:1, bass.ds(g, 1)], min_val=0, max_val=NT - 1)
                dve.wait_ge(products, g + 1)
                after(dve, added, g)
                nc.vector.tensor_tensor(mix[:, bass.ds(tile, 1), :], mix[:, bass.ds(tile, 1), :],
                                        product[:, j:j + 1, :], ALU.add).then_inc(added, 1)

            prepare(0, 0)
            prepare(1, 1)
            add(0, 0)
            with dve.Fori(1, NG // PAIR) as i:
                for j in range(PAIR):
                    prepare(i * PAIR + j, j)
                    add(i * PAIR + j - 1, 1 - j)
            add(NG - 1, 1)

        @block.tensor
        def _(pe):
            def multiply(g, j):
                pe.wait_ge(one_hots, g + 1)
                after(pe, added, g - 1)
                for half in range(2):
                    cols = slice(half * HALF, (half + 1) * HALF)
                    for k in range(SLOTS):
                        for q in range(3):
                            ins = pe.matmul(product[:, j, cols], target[:, j, k, q, :], source[:, j, k, cols],
                                            start=(k == 0 and q == 0), stop=(k == SLOTS - 1 and q == 2))
                ins.then_inc(products, 1)

            multiply(0, 0)
            multiply(1, 1)
            with pe.Fori(1, NG // PAIR) as i:
                for j in range(PAIR):
                    multiply(i * PAIR + j, j)


def pipeline(engine, count, stages, unroll=2):
    high = max(offset for offset, _ in stages)
    low = min(offset for offset, _ in stages)
    begin = unroll - low
    rounds = max(0, (count - high - begin) // unroll)
    if rounds < 2:
        rounds = 0
    end = begin + rounds * unroll

    def single(steps):
        for g in steps:
            for offset, work in stages:
                if 0 <= g + offset < count:
                    work(g + offset, (g + offset) % unroll, (g + offset) // unroll)

    single(range(-high, begin))
    if rounds:
        with engine.Fori(0, rounds) as i:
            for u in range(unroll):
                for offset, work in stages:
                    item = begin + u + offset
                    work(i * unroll + item, item % unroll, i + item // unroll)
    single(range(end, count - low))


class Normaliser:

    def __init__(self, name, nc, c, sb, ps, sem, keep=None, second_eps=None):
        self.nc, self.c, self.keep, self.second_eps = nc, c, keep, second_eps
        self.stats = sb(name + "_stats", [P, 2, 2, 6])
        self.moments = sb(name + "_moments", [P, 2, 2])
        self.spread_eps = sb(name + "_variance_eps", [P, 2, 2])
        self.inverse = sb(name + "_inverse_deviation", [P, 2, 2])
        self.power = sb(name + "_minus_half", [P, 1])
        if second_eps is not None:
            self.once = sb(name + "_once", [P, 2, 2])
            self.second = sb(name + "_second_eps", [P, 1])
            self.second_step = sem(name + "_second_step")
        self.normal = None if keep is not None else sb(name + "_normal", [P, 2, D])
        self.turned_sb = sb(name + "_normal_turned", [P, 2, KT, P])
        self.turned_ps = ps(name + "_normal_turned_ps", [P, 2, KT // 2, P])
        self.power_ready = sem(name + "_minus_half_ready")
        self.stats_ready = sem(name + "_stats_ready")
        self.stats_awaited = sem(name + "_stats_awaited")
        self.moments_ready = sem(name + "_moments_ready")
        self.variance_ready = sem(name + "_variance_ready")
        self.inverse_ready = sem(name + "_inverse_ready")
        self.plain_ready = sem(name + "_plain_ready")
        self.normal_ready = sem(name + "_normal_ready")
        self.turned = sem(name + "_normal_turned")
        self.taken = sem(name + "_normal_taken")
        self.products = sem(name + "_tile_products")

    def tile(self, t, j):
        return self.keep[:, bass.ds(t, 1), :] if self.keep is not None else self.normal[:, j:j + 1, :]

    def vector(self, dve, t, j, quantised=None):
        nc, x = self.nc, self.c.x
        for half in range(2):
            nc.vector.bn_stats(self.stats[:, j, half, :], x[:, bass.ds(t, 1), half * HALF:(half + 1) * HALF]
                               ).then_inc(self.stats_ready, 1)
        dve.wait_ge(self.stats_ready, 2 * t + 2)
        dve.sem_inc(self.stats_awaited, 1)
        nc.vector.bn_aggr(self.moments[:, j, :], self.stats[:, j, :, :]).then_inc(self.moments_ready, 1)
        dve.wait_ge(self.moments_ready, t + 1)
        nc.vector.tensor_scalar(self.spread_eps[:, j, 0:1], self.moments[:, j, 1:2], 1e-5, None, ALU.add
                                ).then_inc(self.variance_ready, 1)
        dve.wait_ge(self.inverse_ready, t + 1)
        if self.keep is None:
            after(dve, self.turned, 2 * (t - 1))
        ready = self.normal_ready if quantised is None else self.plain_ready
        nc.vector.tensor_scalar(self.tile(t, j), x[:, bass.ds(t, 1), :], self.moments[:, j, 0:1],
                                self.inverse[:, j, 0:1], ALU.subtract, ALU.mult).then_inc(ready, 1)
        if quantised is not None:
            dve.wait_ge(self.plain_ready, t + 1)
            quantised.vector(dve, t, self.normal[:, j, :], self.normal[:, j, :])

    def gpsimd(self, pool, t, j):
        pool.wait_ge(self.variance_ready, t + 1)
        if self.second_eps is not None:
            tt = self.nc.gpsimd.tensor_tensor
            once, var = self.once[:, j, 0:1], self.moments[:, j, 1:2]
            twice = self.once[:, j, 1:2]
            link = Link(pool, self.second_step)
            link.count = t * 5
            link(tt(once, self.spread_eps[:, j, 0:1], self.power[:], ALU.pow))
            link(tt(twice, once, once, ALU.mult))
            link(tt(twice, twice, var, ALU.mult))
            link(tt(twice, twice, self.second[:], ALU.add))
            link(tt(twice, twice, self.power[:], ALU.pow))
            tt(self.inverse[:, j, 0:1], once, twice, ALU.mult).then_inc(self.inverse_ready, 1)
            return
        self.nc.gpsimd.tensor_tensor(self.inverse[:, j, 0:1], self.spread_eps[:, j, 0:1], self.power[:], ALU.pow
                                     ).then_inc(self.inverse_ready, 1)

    def tensor(self, pe, t, j):
        pe.wait_ge(self.normal_ready, t + 1)
        for half in range(2):
            after(pe, self.taken, 2 * t + half - 1)
            for k in range(KT // 2):
                b = half * (KT // 2) + k
                cols = slice(b * P, (b + 1) * P)
                source = self.keep[:, t, cols] if self.keep is not None else self.normal[:, j, cols]
                ins = pe.transpose(self.turned_ps[:, half, k, :], source, self.c.ident[:])
            ins.then_inc(self.turned, 1)

    def scalar(self, act, t, j):
        for half in range(2):
            act.wait_ge(self.turned, 2 * t + half + 1)
            if half == 0:
                after(act, self.products, t - 1)
            self.nc.scalar.copy(self.turned_sb[:, j, half * 4:half * 4 + 4, :], self.turned_ps[:, half, :, :]
                                ).then_inc(self.taken, 1)


def apply_mix(nc, c, mix, bias):
    with ExitStack() as ctx:
        sb, ps, sem = pools(nc, ctx)
        norm = Normaliser("mixing", nc, c, sb, ps, sem)
        bias_rows = sb("bias_rows", [P, D])
        product = ps("node_product", [P, 2, D])
        bias_loaded = sem("bias_loaded")
        biased = sem("biased")
        summed = sem("node_summed")
        block = ctx.enter_context(nc.Block())

        @block.sync
        def _(sp):
            sp.dma_start(bias_rows[:], bias.partition_broadcast(P)).then_inc(bias_loaded, 16)

        @block.gpsimd
        def _(pool):
            nc.gpsimd.memset(norm.power[:], -0.5).then_inc(norm.power_ready, 1)
            pool.wait_ge(norm.power_ready, 1)
            pool.wait_ge(bias_loaded, 16)

            def add_bias(t, j, r):
                pool.wait_ge(norm.normal_ready, t + 1)
                tile = c.x[:, bass.ds(t, 1), :]
                nc.gpsimd.tensor_tensor(tile, tile, spread(bias_rows[:], 1, 1), ALU.add).then_inc(biased, 1)

            pipeline(pool, NT, [(1, lambda t, j, r: norm.gpsimd(pool, t, j)), (0, add_bias)])

        @block.vector
        def _(dve):
            def add_product(t, j, r):
                dve.wait_ge(biased, t + 1)
                dve.wait_ge(norm.products, t + 1)
                tile = c.x[:, bass.ds(t, 1), :]
                nc.vector.tensor_tensor(tile, tile, product[:, j:j + 1, :], ALU.add).then_inc(summed, 1)

            pipeline(dve, NT, [(1, lambda t, j, r: norm.vector(dve, t, j)), (0, add_product)])

        @block.scalar
        def _(act):
            pipeline(act, NT, [(0, lambda t, j, r: norm.scalar(act, t, j))])

        @block.tensor
        def _(pe):
            def multiply(t, j, r):
                pe.wait_ge(norm.taken, 2 * t + 2)
                after(pe, summed, t - 1)
                for half in range(2):
                    cols = slice(half * HALF, (half + 1) * HALF)
                    for k in range(KT):
                        ins = pe.matmul(product[:, j, cols], norm.turned_sb[:, j, k, :], mix[:, k, cols],
                                        start=(k == 0), stop=(k == KT - 1))
                ins.then_inc(norm.products, 1)

            pipeline(pe, NT, [(1, lambda t, j, r: norm.tensor(pe, t, j)), (0, multiply)])


def route(nc, c, router_w, router_b, token_rows):
    STEPS = 5
    with ExitStack() as ctx:
        sb, ps, sem = pools(nc, ctx)
        normal = sb("all_normal", [P, NT, D])
        norm = Normaliser("routing", nc, c, sb, ps, sem, keep=normal)
        weight = sb("router_weight", [P, KT, XE])
        bias = sb("router_bias", [P, XE])
        order = sb("expert_order", [P, XE])
        valid = sb("valid", [P, 1])
        logit = sb("logit", [P, 2, XE])
        best = sb("best", [P, 2, 1])
        first = sb("first", [P, 2, XE])
        member = sb("token_member", [P, XE, NT])
        product = ps("logit_product", [P, 2, HALF])
        k = sorting_memory(sb, ps, sem, c, "token", P, XE, NT, XS)
        loaded = sem("router_loaded")
        chosen = sem("choice_step")
        step = sem("token_step")
        placed = sem("tokens_placed")
        sent = sem("tokens_sent")
        block = ctx.enter_context(nc.Block())

        @block.sync
        def _(sp):
            sp.dma_start(weight[:], router_w.rearrange("(k p) e -> p k e", p=P)).then_inc(loaded, 16)
            sp.dma_start(bias[:], router_b.partition_broadcast(P)).then_inc(loaded, 16)

        @block.gpsimd
        def _(pool):
            nc.gpsimd.memset(norm.power[:], -0.5).then_inc(norm.power_ready, 1)
            pool.wait_ge(norm.power_ready, 1)
            pipeline(pool, NT, [(0, lambda t, j, r: norm.gpsimd(pool, t, j))])
            pool.wait_ge(placed, 1)
            for t in range(NT):
                rows = P if t < NT - 1 else LAST
                pool.indirect_dma_start(out=token_rows, out_offset=bass.IndirectOffsetOnAxis(ap=c.token_place[0:rows, t:t + 1], axis=0),
                                        in_=normal[0:rows, t, :], in_offset=None).then_inc(sent, 16)
            pool.wait_ge(sent, 16 * NT)

        @block.scalar
        def _(act):
            pipeline(act, NT, [(0, lambda t, j, r: norm.scalar(act, t, j))])

        @block.tensor
        def _(pe):
            pe.wait_ge(loaded, 32)

            def multiply(t, j, r):
                pe.wait_ge(norm.taken, 2 * t + 2)
                after(pe, chosen, STEPS * (t - 1))
                for b in range(KT):
                    ins = pe.matmul(product[:, j, 0:XE], norm.turned_sb[:, j, b, :], weight[:, b, :],
                                    start=(b == 0), stop=(b == KT - 1))
                ins.then_inc(norm.products, 1)

            norm.tensor(pe, 0, 0)
            for t in range(NT):
                if t + 1 < NT:
                    norm.tensor(pe, t + 1, (t + 1) % 2)
                multiply(t, t % 2, t // 2)
            count_totals(nc, pe, c, k, P, XE)

        @block.vector
        def _(dve):
            link = Link(dve, step)
            link(nc.vector.memset(k.all_one[:], 1.0))
            link(nc.vector.tensor_scalar(order[:], c.iota[:, 0:XE], -1.0, float(XE), ALU.mult, ALU.add))
            link(nc.vector.tensor_scalar(valid[:], c.part[:], float(LAST), None, ALU.is_lt))
            dve.wait_ge(loaded, 32)

            def choose(t, j, r):
                pick = Link(dve, chosen)
                pick.count = t * STEPS
                dve.wait_ge(norm.products, t + 1)
                pick(nc.vector.tensor_tensor(logit[:, j, :], product[:, j, 0:XE], bias[:], ALU.add))
                pick(nc.vector.tensor_reduce(best[:, j, :], logit[:, j, :], AX.X, ALU.max))
                pick(nc.vector.scalar_tensor_tensor(first[:, j, :], logit[:, j, :], best[:, j, :], order[:], ALU.is_ge, ALU.mult))
                pick(nc.vector.tensor_reduce(best[:, j, :], first[:, j, :], AX.X, ALU.max))
                pick(nc.vector.tensor_scalar(member[:, :, bass.ds(t, 1)], spread(order[:], 2, 1), best[:, j, :], None, ALU.is_equal))

            pipeline(dve, NT, [(1, lambda t, j, r: norm.vector(dve, t, j)), (0, choose)])
            link(nc.vector.tensor_scalar(member[:, :, NT - 1], member[:, :, NT - 1], valid[:, 0:1], None, ALU.mult))
            count_positions(nc, dve, link, k, P, member[:], NT, 7, XS, c.slot_expert[:])
            nc.vector.tensor_copy(c.token_place[:], k.position[:]).then_inc(placed, 1)


def run_experts(nc, c, w1, b1, w2, b2, token_rows, expert_rows):
    HB = HID // P
    with ExitStack() as ctx:
        sb, ps, sem = pools(nc, ctx)
        weight1 = sb("expert_weight1", [P, 2, KT, 2 * HID])
        weight2 = sb("expert_weight2", [P, 2, HB, D])
        bias1 = sb("expert_bias1", [1, 2, 2 * HID])
        bias2 = sb("expert_bias2", [1, 2, D])
        token = sb("slot_token", [P, 2, D])
        token_turned = sb("token_turned", [P, 2, KT, P])
        gate = sb("expert_gate", [P, 2, HID])
        hidden = sb("expert_hidden", [P, 2, HID])
        hidden_turned = sb("hidden_turned", [P, 2, HB, P])
        result = sb("expert_result", [P, 2, D])
        turned_ps = ps("token_turned_ps", [P, KT // 2, P])
        hidden_ps = ps("hidden_ps", [P, 2, 2 * HID])
        hidden_turned_ps = ps("hidden_turned_ps", [P, HB, P])
        result_ps = ps("result_ps", [P, 2, HALF])
        token_loaded = [sem(f"token_loaded{j}") for j in range(2)]
        first_loaded = [sem(f"first_loaded{j}") for j in range(2)]
        second_loaded = [sem(f"second_loaded{j}") for j in range(2)]
        tokens_turned = sem("tokens_turned")
        tokens_taken = sem("tokens_taken")
        hiddens = sem("hiddens")
        gates = sem("gates")
        gated = sem("gated")
        hiddens_turned = sem("hiddens_turned")
        hiddens_taken = sem("hiddens_taken")
        results = sem("results")
        results_taken = sem("results_taken")
        results_stored = [sem(f"results_stored{j}") for j in range(2)]
        block = ctx.enter_context(nc.Block())

        @block.sync
        def _(sp):
            def load_first(s, j, r):
                expert = sp.value_load(c.slot_expert[0:1, bass.ds(s, 1)], min_val=0, max_val=XE - 1)
                after(sp, tokens_turned, 2 * (s - 1))
                sp.dma_start(token[:, j, :], token_rows[bass.ds(s * P, P), :]).then_inc(token_loaded[j], 16)
                after(sp, hiddens, s - 1)
                sp.dma_start(weight1[:, j, :, :], w1[bass.ds(expert, 1), :, :].rearrange("e (k p) f -> p (e k) f", p=P)
                             ).then_inc(first_loaded[j], 16)
                sp.dma_start(bias1[:, j, :], b1[bass.ds(expert, 1), :]).then_inc(first_loaded[j], 16)

            def load_second(s, j, r):
                expert = sp.value_load(c.slot_expert[0:1, bass.ds(s, 1)], min_val=0, max_val=XE - 1)
                after(sp, results, 2 * (s - 1))
                sp.dma_start(weight2[:, j, :, :], w2[bass.ds(expert, 1), :, :].rearrange("e (k p) f -> p (e k) f", p=P)
                             ).then_inc(second_loaded[j], 16)
                sp.dma_start(bias2[:, j, :], b2[bass.ds(expert, 1), :]).then_inc(second_loaded[j], 16)

            pipeline(sp, XS, [(1, load_first), (0, load_second)])

        @block.tensor
        def _(pe):
            def turn_token(s, j, r, half):
                if half == 0:
                    pe.wait_ge(token_loaded[j], r * 16 + 16)
                after(pe, tokens_taken, 2 * s + half)
                for k in range(KT // 2):
                    b = half * (KT // 2) + k
                    ins = pe.transpose(turned_ps[:, k, :], token[:, j, b * P:(b + 1) * P], c.ident[:])
                ins.then_inc(tokens_turned, 1)

            def first(s, j, r):
                pe.wait_ge(tokens_taken, 2 * s + 2)
                pe.wait_ge(first_loaded[j], r * 32 + 32)
                after(pe, gated, s - 1)
                for half in range(2):
                    cols = slice(half * HID, (half + 1) * HID)
                    pe.matmul(hidden_ps[:, j, cols], c.ones[0:1, :], bias1[:, j, cols], start=True, stop=False)
                    for k in range(KT):
                        ins = pe.matmul(hidden_ps[:, j, cols], token_turned[:, j, k, :], weight1[:, j, k, cols],
                                        start=False, stop=(k == KT - 1))
                ins.then_inc(hiddens, 1)

            def second(s, j, r):
                pe.wait_ge(gated, s + 1)
                after(pe, hiddens_taken, s)
                for k in range(HB):
                    ins = pe.transpose(hidden_turned_ps[:, k, :], hidden[:, j, k * P:(k + 1) * P], c.ident[:])
                ins.then_inc(hiddens_turned, 1)
                pe.wait_ge(second_loaded[j], r * 32 + 32)
                pe.wait_ge(hiddens_taken, s + 1)
                for half in range(2):
                    cols = slice(half * HALF, (half + 1) * HALF)
                    after(pe, results_taken, 2 * s + half - 1)
                    pe.matmul(result_ps[:, half, :], c.ones[0:1, :], bias2[:, j, cols], start=True, stop=False)
                    for k in range(HB):
                        ins = pe.matmul(result_ps[:, half, :], hidden_turned[:, j, k, :], weight2[:, j, k, cols],
                                        start=False, stop=(k == HB - 1))
                    ins.then_inc(results, 1)

            pipeline(pe, XS, [(2, lambda s, j, r: turn_token(s, j, r, 0)), (2, lambda s, j, r: turn_token(s, j, r, 1)),
                              (1, first), (0, second)])

        @block.scalar
        def _(act):
            def take_token(s, j, r):
                for half in range(2):
                    act.wait_ge(tokens_turned, 2 * s + half + 1)
                    after(act, hiddens, s - 1)
                    nc.scalar.copy(token_turned[:, j, half * 4:half * 4 + 4, :], turned_ps[:]).then_inc(tokens_taken, 1)

            def squash(s, j, r):
                act.wait_ge(hiddens, s + 1)
                after(act, gated, s - 1)
                nc.scalar.activation(gate[:, j, :], hidden_ps[:, j, HID:2 * HID], ACT.Sigmoid).then_inc(gates, 1)

            def take_result(s, j, r):
                after(act, results_stored[j], r * 16)
                for half in range(2):
                    act.wait_ge(results, 2 * s + half + 1)
                    nc.scalar.copy(result[:, j, half * HALF:(half + 1) * HALF], result_ps[:, half, :]).then_inc(results_taken, 1)
                act.wait_ge(results_taken, 2 * s + 2)
                act.dma_start(expert_rows[bass.ds(s * P, P), :], result[:, j, :]).then_inc(results_stored[j], 16)

            pipeline(act, XS, [(2, take_token), (1, squash), (0, take_result)])
            for j in range(2):
                act.wait_ge(results_stored[j], 16 * len(range(j, XS, 2)))

        @block.vector
        def _(dve):
            def multiply(s, j, r):
                dve.wait_ge(gates, s + 1)
                after(dve, hiddens_turned, s - 1)
                nc.vector.tensor_tensor(hidden[:, j, :], hidden_ps[:, j, 0:HID], gate[:, j, :], ALU.mult).then_inc(gated, 1)

            def take_hidden(s, j, r):
                dve.wait_ge(hiddens_turned, s + 1)
                after(dve, results, 2 * (s - 1))
                nc.vector.tensor_copy(hidden_turned[:, j, :, :], hidden_turned_ps[:]).then_inc(hiddens_taken, 1)

            pipeline(dve, XS, [(1, multiply), (0, take_hidden)])


def attention_inputs(nc, c, att, w_down, w_l, w_r, rms_w, expert_rows, left_rows, both, right_parts, best, total):
    HB = HD // P
    with ExitStack() as ctx:
        sb, ps, sem = pools(nc, ctx)
        norm = Normaliser("projecting", nc, c, sb, ps, sem, second_eps=1e-6)
        down = sb("down_weight", [P, KT, HD])
        scale = sb("rms_weight", [P, KT])
        sides = sb("side_weights", [P, HB, 2 * HD])
        gathered = sb("expert_gathered", [P, 2, D])
        narrow = sb("narrow_turned", [P, 2, HB, P])
        score = sb("self_score", [P, 2, HD])
        right_rest = sb("right_rest", [P, 1, HD])
        narrow_ps = ps("narrow_ps", [P, 2, HB, HALF // 2])
        sides_ps = ps("sides_ps", [P, 2, HALF])
        loaded = sem("projection_loaded")
        scaled = sem("down_scaled")
        rows_here = [sem(f"expert_rows_here{j}") for j in range(2)]
        updated = sem("nodes_updated")
        update_awaited = sem("update_awaited")
        narrow_taken = sem("narrow_taken")
        sided = sem("sided")
        sides_taken = sem("sides_taken")
        stored = sem("left_rows_stored")
        scored = sem("self_scored")
        parted = sem("right_parted")
        block = ctx.enter_context(nc.Block())

        @block.sync
        def _(sp):
            sp.dma_start(scale[:], rms_w.rearrange("(k p) -> p k", p=P), allow_slow_non_contiguous=True).then_inc(loaded, 16)
            sp.dma_start(down[:], w_down.rearrange("(k p) f -> p k f", p=P)).then_inc(loaded, 16)
            sp.dma_start(sides[:, :, 0:HD], w_l.rearrange("(k p) f -> p k f", p=P)).then_inc(loaded, 16)
            sp.dma_start(sides[:, :, HD:2 * HD], w_r.rearrange("(k p) f -> p k f", p=P)).then_inc(loaded, 16)
            sp.dma_start(c.att_rows[:], att.rearrange("h d -> (h d)").partition_broadcast(P)).then_inc(loaded, 16)
            for t in range(NT):
                sp.wait_ge(sides_taken, t + 1)
                sp.dma_start(left_rows[t * P:(t + 1) * P, :], both[:, t, 0:HD]).then_inc(stored, 16)
            sp.wait_ge(stored, 16 * NT)

        @block.gpsimd
        def _(pool):
            nc.gpsimd.memset(norm.power[:], -0.5).then_inc(norm.power_ready, 1)
            nc.gpsimd.memset(norm.second[:], norm.second_eps).then_inc(norm.power_ready, 1)
            pool.wait_ge(norm.power_ready, 2)
            for t in range(NT + 1):
                if t < NT:
                    after(pool, updated, t - 1)
                    pool.indirect_dma_start(out=gathered[:, t % 2, :], out_offset=None, in_=expert_rows,
                                            in_offset=bass.IndirectOffsetOnAxis(ap=c.token_place[:, t:t + 1], axis=0)
                                            ).then_inc(rows_here[t % 2], 16)
                if t >= 1:
                    norm.gpsimd(pool, t - 1, (t - 1) % 2)

        @block.vector
        def _(dve):
            dve.wait_ge(loaded, 80)
            for k in range(KT):
                ins = nc.vector.tensor_scalar(down[:, k, :], down[:, k, :], scale[:, k:k + 1], None, ALU.mult)
            ins.then_inc(scaled, 1)

            def update(t, j, r):
                dve.wait_ge(rows_here[j], r * 16 + 16)
                tile = c.x[:, bass.ds(t, 1), :]
                nc.vector.tensor_tensor(tile, tile, gathered[:, j:j + 1, :], ALU.add).then_inc(updated, 1)
                dve.wait_ge(updated, t + 1)
                dve.sem_inc(update_awaited, 1)
                norm.vector(dve, t, j)

            def take(t, j, r):
                dve.wait_ge(sided, t + 1)
                nc.vector.tensor_scalar(both[:, bass.ds(t, 1), :], sides_ps[:, j:j + 1, :], 1.0, None, ALU.mult).then_inc(sides_taken, 1)
                dve.wait_ge(sides_taken, t + 1)
                step = Link(dve, parted)
                step.count = 5 * t
                rest = right_rest[:]
                for q in range(3):
                    part = right_parts[:, bass.ds(t, 1), q * HD:(q + 1) * HD]
                    source = both[:, bass.ds(t, 1), HD:2 * HD] if q == 0 else rest
                    step(nc.vector.tensor_scalar(part, source, 1.0, None, ALU.mult))
                    if q < 2:
                        step(nc.vector.tensor_tensor(rest, source, part, ALU.subtract))

            pipeline(dve, NT, [(1, update), (0, take)])
            link = Link(dve, scored)
            for t in range(NT):
                j = t % 2
                link(nc.vector.tensor_tensor(score[:, j, :], both[:, t, 0:HD], both[:, t, HD:2 * HD], ALU.add))
                link(nc.vector.scalar_tensor_tensor(score[:, j, :], score[:, j, :], 0.2, score[:, j, :], ALU.mult, ALU.max))
                link(nc.vector.tensor_tensor(score[:, j, :], score[:, j, :], c.att_rows[:], ALU.mult))
                link(nc.vector.tensor_reduce(best[:, t, :], score[:, j, :].rearrange("p (h d) -> p h d", h=NH), AX.X, ALU.add))
            nc.vector.tensor_copy(total[:, :, :, 0:HW], both[:, :, 0:HD].rearrange("p t (h d) -> p t h d", h=NH))
            nc.vector.memset(total[:, :, :, HW:HW1], 1.0)

        @block.scalar
        def _(act):
            def take_narrow(t, j, r):
                act.wait_ge(norm.products, t + 1)
                after(act, sided, t - 1)
                nc.scalar.copy(narrow[:, j, :, :], narrow_ps[:, j, :, 0:P]).then_inc(narrow_taken, 1)

            pipeline(act, NT, [(1, lambda t, j, r: norm.scalar(act, t, j)), (0, take_narrow)])

        @block.tensor
        def _(pe):
            pe.wait_ge(scaled, 1)

            def narrow_down(t, j, r):
                pe.wait_ge(norm.taken, 2 * t + 2)
                after(pe, narrow_taken, t - 1)
                for m in range(HB):
                    for k in range(KT):
                        ins = pe.matmul(narrow_ps[:, j, m, 0:P], down[:, k, m * P:(m + 1) * P], norm.turned_sb[:, j, k, :],
                                        start=(k == 0), stop=(k == KT - 1))
                ins.then_inc(norm.products, 1)

            def make_sides(t, j, r):
                pe.wait_ge(narrow_taken, t + 1)
                after(pe, sides_taken, t - 1)
                for m in range(HB):
                    ins = pe.matmul(sides_ps[:, j, :], narrow[:, j, m, :], sides[:, m, :], start=(m == 0), stop=(m == HB - 1))
                ins.then_inc(sided, 1)

            pipeline(pe, NT, [(1, lambda t, j, r: norm.tensor(pe, t, j)), (0, narrow_down), (0, make_sides)])


def attend(nc, c, left_rows, both, right_parts, best, total):
    B, B3, B2 = 6, 3, 2
    with ExitStack() as ctx:
        sb, ps, sem = pools(nc, ctx)
        index = sb("gather_index", [P, B, SLOTS], I32)
        left = sb("left_of_edge", [P, B, SLOTS, HD])
        right = sb("right_of_tile", [P, B3, 3 * HD], BF16)
        member = sb("edge_member", [P, B, SLOTS, P])
        outside = sb("edge_outside", [P, B, SLOTS, P], BF16)
        member_turned = sb("edge_member_turned", [P, B, SLOTS, P], BF16)
        leaky = sb("leaky_message", [P, B2, SLOTS, HD])
        weighted = sb("weighted_message", [P, B2, SLOTS, HD])
        score = sb("edge_score", [P, B, GH])
        score_rest = sb("edge_score_rest", [P, B, GH])
        score_parts = sb("edge_score_parts", [P, B, 3, GH], BF16)
        score_rows = sb("edge_score_rows", [3 * GH, B, P], BF16)
        slot_best = sb("slot_best", [P, B, NH, SLOTS])
        group_best = sb("group_best", [P, B, NH])
        new_best = sb("new_best", [P, B, NH])
        best_rest = sb("new_best_rest", [P, B, NH])
        best_parts = sb("new_best_parts", [P, B, 3, NH], BF16)
        fade = sb("fade", [P, B, NH])
        below = sb("score_below_best", [P, B, GH])
        value = sb("edge_value", [P, B2, SLOTS, NH, HW1])
        z_ps = ps("message_ps", [P, SLOTS, HD])
        spread_ps = ps("score_spread_ps", [P, 2, NH, P])
        turned_ps = ps("member_turned_ps", [P, SLOTS, 2 * P], BF16)
        rows_ps = ps("score_rows_ps", [3 * GH, 2 * HALF], BF16)
        best_ps = ps("best_of_edge_ps", [P, HALF])
        sum_ps = ps("edge_sum_ps", [P, HALF])
        S = Shared()
        S.indexed = sem("index_ready")
        S.index_awaited = sem("index_awaited")
        S.scores_awaited = sem("scores_awaited")
        S.members = sem("members_ready")
        S.outsides = sem("outsides_ready")
        S.turned = sem("members_turned")
        S.turned_taken = sem("members_turned_taken")
        S.messages = sem("messages_ready")
        S.positives = sem("positives_ready")
        S.leaky = sem("leaky_ready")
        S.weighted = sem("weighted_ready")
        S.score_step = sem("score_step")
        S.rows = sem("score_rows_ready")
        S.rows_taken = sem("score_rows_taken")
        S.spread = sem("scores_spread")
        S.slot_maxed = sem("slots_maxed")
        S.best_step = sem("best_step")
        S.best_edges = sem("best_of_edges_ready")
        S.belows = sem("belows_ready")
        S.fades = sem("fades_ready")
        S.exps = sem("exponentials_ready")
        S.values = sem("values_ready")
        S.sums = sem("sums_ready")
        S.rescaled = sem("totals_rescaled")
        S.added = sem("totals_added")
        here = [sem(f"left_here{j}") for j in range(B)]
        SCORE_STEPS, BEST_STEPS = 6, 9
        block = ctx.enter_context(nc.Block())

        @block.gpsimd
        def _(pool):
            def gather(g, j, r):
                after(pool, S.values, g - B + 1)
                nc.gpsimd.tensor_copy(index[:, j, :], c.source_i[:, bass.ds(g * SLOTS, SLOTS)]).then_inc(S.indexed, 1)
                pool.wait_ge(S.indexed, g + 1)
                pool.sem_inc(S.index_awaited, 1)
                for k in range(SLOTS):
                    pool.indirect_dma_start(out=left[:, j, k, :], out_offset=None, in_=left_rows,
                                            in_offset=bass.IndirectOffsetOnAxis(ap=index[:, j, k:k + 1], axis=0)
                                            ).then_inc(here[j], 16)

            def weigh(g, j, r):
                pool.wait_ge(S.leaky, g + 1)
                nc.gpsimd.tensor_tensor(weighted[:, j % B2, :, :], leaky[:, j % B2, :, :], spread(c.att_rows[:], 1, SLOTS),
                                        ALU.mult).then_inc(S.weighted, 1)

            pipeline(pool, NG, [(3, gather), (2, weigh)], unroll=B)

        @block.vector
        def _(dve):
            def tile_of(g):
                return dve.value_load(c.group_tile[0:1, bass.ds(g, 1)], min_val=0, max_val=NT - 1)

            def max_of_slots(g, j, half):
                for k in (2 * half, 2 * half + 1):
                    dve.wait_ge(S.spread, SLOTS * g + k + 1)
                    nc.vector.tensor_reduce(slot_best[:, j, :, k], spread_ps[:, k % 2, :, :], AX.X, ALU.max
                                            ).then_inc(S.slot_maxed, 1)

            def leak(g, j, r):
                dve.wait_ge(S.positives, g + 1)
                after(dve, S.weighted, g - B2 + 1)
                nc.vector.scalar_tensor_tensor(leaky[:, j % B2, :, :], z_ps[:], 0.2, weighted[:, j % B2, :, :], ALU.mult, ALU.add
                                               ).then_inc(S.leaky, 1)

            def raise_best(g, j, r):
                tile = tile_of(g)
                step = Link(dve, S.best_step)
                step.count = g * BEST_STEPS
                dve.wait_ge(S.slot_maxed, SLOTS * g + SLOTS)
                step(nc.vector.tensor_reduce(group_best[:, j, :], slot_best[:, j, :, :], AX.X, ALU.max))
                mine, new, rest = best[:, bass.ds(tile, 1), :], new_best[:, j:j + 1, :], best_rest[:, j, :]
                step(nc.vector.tensor_tensor(new, group_best[:, j:j + 1, :], mine, ALU.max))
                nc.vector.tensor_tensor(fade[:, j:j + 1, :], mine, new, ALU.subtract).then_inc(S.best_step, 1)
                step.count += 1
                step(nc.vector.tensor_copy(best_parts[:, j, 0, :], new_best[:, j, :]))
                step(nc.vector.tensor_tensor(rest, new_best[:, j, :], best_parts[:, j, 0, :], ALU.subtract))
                step(nc.vector.tensor_copy(best_parts[:, j, 1, :], rest))
                step(nc.vector.tensor_tensor(rest, rest, best_parts[:, j, 1, :], ALU.subtract))
                step(nc.vector.tensor_copy(best_parts[:, j, 2, :], rest))
                nc.vector.tensor_scalar(mine, new, 1.0, None, ALU.mult).then_inc(S.best_step, 1)

            def accumulate(g, j, r):
                tile = tile_of(g)
                dve.wait_ge(S.fades, g + 1)
                after(dve, S.added, g)
                mine = total[:, bass.ds(tile, 1), :, :].rearrange("p t h d -> p (t h) d")
                nc.vector.tensor_tensor(mine, mine, spread(fade[:, j, :], 2, HW1), ALU.mult).then_inc(S.rescaled, 1)
                dve.wait_ge(S.rescaled, g + 1)
                dve.wait_ge(S.sums, g + 1)
                nc.vector.tensor_tensor(mine, mine, sum_ps[:, 0:NH * HW1].rearrange("p (h d) -> p h d", h=NH), ALU.add
                                        ).then_inc(S.added, 1)

            def prepare(g, j, r):
                tile = tile_of(g)
                after(dve, S.sums, g - B + 1)
                after(dve, S.messages, g - B3 + 1)
                for k in range(SLOTS):
                    nc.vector.tensor_scalar(member[:, j, k, :], c.iota[:, 0:P], c.edges[:, bass.ds(g * SLOTS + k, 1), 1],
                                            None, ALU.is_equal)
                nc.vector.tensor_scalar(right[:, j % B3:j % B3 + 1, :], right_parts[:, bass.ds(tile, 1), :], 1.0, None, ALU.mult
                                        ).then_inc(S.members, 1)

            def lower(g, j, r):
                dve.wait_ge(S.best_edges, g + 1)
                nc.vector.tensor_tensor(below[:, j, :], score[:, j, :], best_ps[:, 0:GH], ALU.subtract).then_inc(S.belows, 1)
                dve.wait_ge(S.belows, 2 * g + 1)
                nc.vector.tensor_scalar(below[:, j, :], below[:, j, :], 0.0, None, ALU.min).then_inc(S.belows, 1)

            def score_edges(g, j, r):
                step = Link(dve, S.score_step)
                step.count = g * SCORE_STEPS
                dve.wait_ge(S.weighted, g + 1)
                rest = score_rest[:, j, :]
                step(nc.vector.tensor_reduce(score[:, j, :], weighted[:, j % B2, :, :].rearrange("p k (h d) -> p (k h) d", h=NH),
                                             AX.X, ALU.add))
                step(nc.vector.tensor_copy(score_parts[:, j, 0, :], score[:, j, :]))
                step(nc.vector.tensor_tensor(rest, score[:, j, :], score_parts[:, j, 0, :], ALU.subtract))
                step(nc.vector.tensor_copy(score_parts[:, j, 1, :], rest))
                step(nc.vector.tensor_tensor(rest, rest, score_parts[:, j, 1, :], ALU.subtract))
                nc.vector.tensor_copy(score_parts[:, j, 2, :], rest).then_inc(S.score_step, 1)

            pipeline(dve, NG, [(0, lambda g, j, r: max_of_slots(g, j, 0)), (1, score_edges),
                               (0, lambda g, j, r: max_of_slots(g, j, 1)), (0, raise_best), (2, leak), (-2, accumulate),
                               (4, prepare), (0, lower)], unroll=B)

        @block.scalar
        def _(act):
            def make_values(g, j, r):
                act.wait_ge(S.exps, g + 1)
                for k in range(SLOTS):
                    for h in range(NH):
                        ins = nc.scalar.mul(value[:, j % B2, k, h, 0:HW], left[:, j, k, h * HW:(h + 1) * HW],
                                            value[:, j % B2, k, h, HW:HW1])
                ins.then_inc(S.values, 1)

            def take_positive(g, j, r):
                act.wait_ge(S.messages, g + 1)
                after(act, S.score_step, SCORE_STEPS * (g - B2) + 1)
                nc.scalar.activation(weighted[:, j % B2, :, :], z_ps[:], ACT.Relu, scale=0.8).then_inc(S.positives, 1)

            def take_member(g, j, r):
                act.wait_ge(S.turned, g + 1)
                after(act, S.best_edges, g - B + 1)
                nc.scalar.activation(member_turned[:, j, :, :], turned_ps[:, :, 0:P], ACT.Copy, bias=1.0
                                     ).then_inc(S.turned_taken, 1)

            def leave_members(g, j, r):
                act.wait_ge(S.members, g + 1)
                after(act, S.spread, SLOTS * (g - B + 1))
                nc.scalar.activation(outside[:, j, :, :], member[:, j, :, :], ACT.Copy, bias=-1.0).then_inc(S.outsides, 1)

            def exponentials(g, j, r):
                act.wait_ge(S.best_step, BEST_STEPS * g + 3)
                nc.scalar.activation(fade[:, j, :], fade[:, j, :], ACT.Exp).then_inc(S.fades, 1)
                act.wait_ge(S.belows, 2 * g + 2)
                after(act, S.sums, g - B2 + 1)
                nc.scalar.activation(value[:, j % B2, :, :, HW].rearrange("p k h -> p (k h)"), below[:, j, :], ACT.Exp
                                     ).then_inc(S.exps, 1)

            def take_rows(g, j, r):
                act.wait_ge(S.rows, g + 1)
                nc.scalar.copy(score_rows[:, j, :], rows_ps[:, 0:P]).then_inc(S.rows_taken, 1)

            pipeline(act, NG, [(-1, make_values), (2, take_positive), (1, take_rows), (3, take_member), (4, leave_members),
                               (0, exponentials)], unroll=B)

        @block.tensor
        def _(pe):
            def spread_scores(g, j, half):
                if half == 0:
                    pe.wait_ge(S.rows_taken, g + 1)
                for k in (2 * half, 2 * half + 1):
                    after(pe, S.slot_maxed, SLOTS * g + k - 1)
                    pe.matmul(spread_ps[:, k % 2, :, :], outside[:, j, k, :], c.big_ident[:], start=True, stop=False,
                              skip_group_check=True)
                    for h in range(NH):
                        ins = pe.matmul(spread_ps[:, k % 2, h, :], c.row_select[:, k * NH + h, :], score_rows[:, j, :],
                                        start=False, stop=(h == NH - 1), skip_group_check=True)
                    ins.then_inc(S.spread, 1)

            def make_messages(g, j, r):
                pe.wait_ge(S.turned_taken, g + 1)
                pe.wait_ge(here[j], r * SLOTS * 16 + SLOTS * 16)
                after(pe, S.leaky, g)
                for k in range(SLOTS):
                    for q in range(3):
                        pe.matmul(z_ps[:, k, :], member_turned[:, j, k, :], right[:, j % B3, q * HD:(q + 1) * HD],
                                  start=(q == 0), stop=False)
                    ins = pe.matmul(z_ps[:, k, :], c.ident[:], left[:, j, k, :], start=False, stop=True)
                ins.then_inc(S.messages, 1)

            def turn_member(g, j, r):
                pe.wait_ge(S.outsides, g + 1)
                after(pe, S.turned_taken, g)
                for k in range(SLOTS):
                    ins = pe.transpose(turned_ps[:, k, 0:P], outside[:, j, k, :], c.ident_b[:])
                ins.then_inc(S.turned, 1)

            def bring_best(g, j, r):
                pe.wait_ge(S.best_step, BEST_STEPS * g + 8)
                after(pe, S.belows, 2 * g - 1)
                for k in range(SLOTS):
                    for q in range(3):
                        ins = pe.matmul(best_ps[:, k * NH:(k + 1) * NH], member_turned[:, j, k, :], best_parts[:, j, q, :],
                                        start=(q == 0), stop=(q == 2))
                ins.then_inc(S.best_edges, 1)

            def sum_up(g, j, r):
                pe.wait_ge(S.values, g + 1)
                after(pe, S.added, g)
                for k in range(SLOTS):
                    ins = pe.matmul(sum_ps[:, 0:NH * HW1], member[:, j, k, :],
                                    value[:, j % B2, k, :, :].rearrange("p h d -> p (h d)"), start=(k == 0), stop=(k == SLOTS - 1))
                ins.then_inc(S.sums, 1)

            def turn_scores(g, j, r):
                pe.wait_ge(S.score_step, SCORE_STEPS * g + SCORE_STEPS)
                after(pe, S.rows_taken, g)
                pe.sem_inc(S.scores_awaited, 1)
                pe.transpose(rows_ps[:, 0:P], score_parts[:, j, :, :].rearrange("p q r -> p (q r)"), c.ident_b[:]
                             ).then_inc(S.rows, 1)

            pipeline(pe, NG, [(0, lambda g, j, r: spread_scores(g, j, 0)), (2, make_messages),
                              (0, lambda g, j, r: spread_scores(g, j, 1)), (1, turn_scores), (-1, sum_up),
                              (3, turn_member), (0, bring_best)], unroll=B)


def attention_output(nc, c, w_up, total):
    HB = HD // P
    with ExitStack() as ctx:
        sb, ps, sem = pools(nc, ctx)
        up = sb("up_weight", [P, HB, D])
        denominator = sb("denominator", [P, 2, NH])
        mean = sb("attention_mean", [P, 2, NH, HW])
        turned = sb("attention_turned", [P, 2, HB, P])
        turned_ps = ps("attention_turned_ps", [P, 2, HALF])
        product = ps("attention_product", [P, 2, D])
        loaded = sem("up_loaded")
        divided = sem("divide_step")
        means = sem("attention_means")
        turns = sem("attention_turns")
        taken = sem("attention_taken")
        products = sem("attention_products")
        summed = sem("attention_summed")
        block = ctx.enter_context(nc.Block())

        @block.sync
        def _(sp):
            sp.dma_start(up[:], w_up.rearrange("(k p) f -> p k f", p=P)).then_inc(loaded, 16)

        @block.vector
        def _(dve):
            def divide(t, j, r):
                link = Link(dve, divided)
                link.count = t * 2
                link(nc.vector.tensor_scalar(denominator[:, j, :], total[:, bass.ds(t, 1), :, HW], 1e-16, None, ALU.add))
                link(nc.vector.reciprocal(denominator[:, j, :], denominator[:, j, :]))
                after(dve, turns, t - 1)
                nc.vector.tensor_tensor(mean[:, j, :, :], total[:, bass.ds(t, 1), :, 0:HW].rearrange("p t h d -> p (t h) d"),
                                        spread(denominator[:, j, :], 2, HW), ALU.mult).then_inc(means, 1)

            def add_product(t, j, r):
                dve.wait_ge(products, t + 1)
                tile = c.x[:, bass.ds(t, 1), :]
                nc.vector.tensor_tensor(tile, tile, product[:, j:j + 1, :], ALU.add).then_inc(summed, 1)

            pipeline(dve, NT, [(1, divide), (0, add_product)])

        @block.scalar
        def _(act):
            def take(t, j, r):
                act.wait_ge(turns, t + 1)
                after(act, products, t - 1)
                nc.scalar.copy(turned[:, j, :, :], turned_ps[:, j, 0:HD].rearrange("p (m e) -> p m e", m=HB)).then_inc(taken, 1)

            pipeline(act, NT, [(0, take)])

        @block.tensor
        def _(pe):
            pe.wait_ge(loaded, 16)

            def turn(t, j, r):
                pe.wait_ge(means, t + 1)
                after(pe, taken, t - 1)
                flat = mean[:, j, :, :].rearrange("p h d -> p (h d)")
                for m in range(HB):
                    ins = pe.transpose(turned_ps[:, j, m * P:(m + 1) * P], flat[:, m * P:(m + 1) * P], c.ident[:])
                ins.then_inc(turns, 1)

            def multiply(t, j, r):
                pe.wait_ge(taken, t + 1)
                after(pe, summed, t - 1)
                for half in range(2):
                    cols = slice(half * HALF, (half + 1) * HALF)
                    for m in range(HB):
                        ins = pe.matmul(product[:, j, cols], turned[:, j, m, :], up[:, m, cols], start=(m == 0), stop=(m == HB - 1))
                ins.then_inc(products, 1)

            pipeline(pe, NT, [(1, turn), (0, multiply)])


class Quantiser:

    VECTOR = 14

    def __init__(self, name, nc, sb, sem, width):
        self.nc, self.width, self.blocks = nc, width, width // QB
        self.scale = sb(name + "_scale", [P, self.blocks])
        self.inverse = sb(name + "_inverse", [P, self.blocks])
        self.size = sb(name + "_size", [P, width])
        self.sign = sb(name + "_sign", [P, width])
        self.level = sb(name + "_level", [P, width])
        self.step = sem(name + "_step")
        self.signs = sem(name + "_signs")
        self.done = sem(name + "_done")

    def scalar(self, act, n, source, rows=P):
        after(act, self.done, n)
        self.nc.scalar.activation(self.sign[0:rows, :], source, ACT.Sign).then_inc(self.signs, 1)

    def vector(self, dve, n, source, target, rows=P):
        v = self.nc.vector
        blocks = lambda ap: ap.rearrange("p (b q) -> p b q", q=QB)
        scale, inverse = self.scale[0:rows, :], self.inverse[0:rows, :]
        size, level, sign = self.size[0:rows, :], self.level[0:rows, :], self.sign[0:rows, :]
        link = Link(dve, self.step)
        link.count = n * self.VECTOR
        after(dve, self.done, n)
        link(v.tensor_reduce(scale, blocks(source), AX.X, ALU.max, apply_absolute_value=True))
        link(v.tensor_scalar(scale, scale, 1.0 / 6.0, 1e-12, ALU.mult, ALU.max))
        link(v.reciprocal(inverse, scale))
        dve.wait_ge(self.signs, n + 1)
        link(v.tensor_tensor(size, source, sign, ALU.mult))
        link(v.tensor_tensor(blocks(size), blocks(size), spread(inverse, 2, QB), ALU.mult))
        link(v.tensor_scalar(level, size, 5.0, 2.0, ALU.is_gt, ALU.mult))
        link(v.scalar_tensor_tensor(level, size, 3.5, level, ALU.is_gt, ALU.add))
        link(v.scalar_tensor_tensor(level, size, 2.5, level, ALU.is_gt, ALU.add))
        link(v.tensor_scalar(level, level, 2.0, None, ALU.mult))
        for bound in (1.75, 1.25, 0.75, 0.25):
            link(v.scalar_tensor_tensor(level, size, bound, level, ALU.is_gt, ALU.add))
        link(v.scalar_tensor_tensor(level, level, 0.5, sign, ALU.mult, ALU.mult))
        v.tensor_tensor(blocks(target), blocks(level), spread(scale, 2, QB), ALU.mult).then_inc(self.done, 1)


def quantise_weights(nc, c, q_gate, q_up, q_down, in_turned, down_turned):
    FB = -(-FF // P)
    tiles = [(w, n, min(P, FF - n * P)) for w in range(2) for n in range(FB)]
    with ExitStack() as ctx:
        sb, ps, sem = pools(nc, ctx)
        raw = sb("raw_weight", [P, 2, D])
        raw_down = sb("raw_down", [P, 2, FF])
        level = sb("weight_level", [P, 2, D])
        level_down = sb("down_level", [P, 2, FF])
        wide = Quantiser("weight_quantiser", nc, sb, sem, D)
        thin = Quantiser("down_quantiser", nc, sb, sem, FF)
        turned_ps = ps("weight_turned_ps", [P, 2, 2, KT // 2, P])
        down_ps = ps("down_turned_ps", [P, 2, HALF])
        here = [sem(f"raw_weight_here{j}") for j in range(2)]
        down_here = [sem(f"raw_down_here{j}") for j in range(2)]
        turned = sem("weights_turned")
        taken = sem("weights_taken")
        down_done = sem("down_turned")
        down_taken = sem("down_taken")
        block = ctx.enter_context(nc.Block())

        def take(dve, n):
            w, b, rows = tiles[n]
            dve.wait_ge(turned, n + 1)
            first = w * FF + b * P
            nc.vector.tensor_copy(in_turned[:, :, first:first + rows],
                                  turned_ps[:, n % 2, :, :, 0:rows].rearrange("p h k r -> p (h k) r")).then_inc(taken, 1)

        def take_down(dve, n):
            dve.wait_ge(down_done, n + 1)
            for b in range(FB):
                rows = min(P, FF - b * P)
                ins = nc.vector.tensor_copy(down_turned[0:rows, b, n * P:(n + 1) * P], down_ps[0:rows, n % 2, b * P:(b + 1) * P])
            ins.then_inc(down_taken, 1)

        @block.sync
        def _(sp):
            for n, (w, b, rows) in enumerate(tiles):
                after(sp, wide.done, n - 1)
                sp.dma_start(raw[0:rows, n % 2, :], (q_gate, q_up)[w][b * P:b * P + rows, :]).then_inc(here[n % 2], 16)
            for n in range(KT):
                after(sp, thin.done, n - 1)
                sp.dma_start(raw_down[:, n % 2, :], q_down[n * P:(n + 1) * P, :]).then_inc(down_here[n % 2], 16)

        @block.scalar
        def _(act):
            for n, (w, b, rows) in enumerate(tiles):
                act.wait_ge(here[n % 2], 16 * (n // 2 + 1))
                wide.scalar(act, n, raw[0:rows, n % 2, :], rows)
            for n in range(KT):
                act.wait_ge(down_here[n % 2], 16 * (n // 2 + 1))
                thin.scalar(act, n, raw_down[:, n % 2, :])

        @block.vector
        def _(dve):
            for n, (w, b, rows) in enumerate(tiles):
                dve.wait_ge(here[n % 2], 16 * (n // 2 + 1))
                after(dve, turned, n - 1)
                wide.vector(dve, n, raw[0:rows, n % 2, :], level[0:rows, n % 2, :], rows)
                if n:
                    take(dve, n - 1)
            take(dve, len(tiles) - 1)
            for n in range(KT):
                dve.wait_ge(down_here[n % 2], 16 * (n // 2 + 1))
                after(dve, down_done, n - 1)
                thin.vector(dve, n, raw_down[:, n % 2, :], level_down[:, n % 2, :])
                if n:
                    take_down(dve, n - 1)
            take_down(dve, KT - 1)

        @block.tensor
        def _(pe):
            for n, (w, b, rows) in enumerate(tiles):
                pe.wait_ge(wide.done, n + 1)
                after(pe, taken, n - 1)
                for k in range(KT):
                    ins = pe.transpose(turned_ps[:, n % 2, k // 4, k % 4, 0:rows], level[0:rows, n % 2, k * P:(k + 1) * P],
                                       c.ident[0:rows, 0:rows])
                ins.then_inc(turned, 1)
            for n in range(KT):
                pe.wait_ge(thin.done, n + 1)
                after(pe, down_taken, n - 1)
                for b in range(FB):
                    cols = min(P, FF - b * P)
                    ins = pe.transpose(down_ps[0:cols, n % 2, b * P:(b + 1) * P], level_down[:, n % 2, b * P:b * P + cols], c.ident[:])
                ins.then_inc(down_done, 1)


def quantised_feed_forward(nc, c, q_gate, q_up, q_down, out):
    FB = -(-FF // P)
    with ExitStack() as ctx:
        sb, ps, sem = pools(nc, ctx)
        in_turned = sb("in_turned", [P, KT, 2 * FF])
        down_turned = sb("down_weight_turned", [P, FB, D])
        quantise_weights(nc, c, q_gate, q_up, q_down, in_turned, down_turned)
        norm = Normaliser("last", nc, c, sb, ps, sem)
        first = Quantiser("node_quantiser", nc, sb, sem, D)
        norm.normal_ready = first.done
        second = Quantiser("hidden_quantiser", nc, sb, sem, FF)
        gate = sb("last_gate", [P, 2, FF])
        hidden = sb("last_hidden", [P, 2, FF])
        level = sb("hidden_level", [P, 2, FF])
        hidden_turned = sb("last_hidden_turned", [P, 2, FB, P])
        gate_ps = ps("last_gate_ps", [P, HALF])
        up_ps = ps("last_up_ps", [P, HALF])
        hidden_ps = ps("last_hidden_ps", [P, HALF])
        result_ps = ps("last_result_ps", [P, 2, HALF])
        plain = sem("last_plain")
        gated = sem("last_gated")
        sized = sem("last_sized")
        hiddens = sem("last_hiddens")
        turns = sem("last_turns")
        taken = sem("last_hidden_taken")
        results = sem("last_results")
        summed = sem("last_summed")
        stored = sem("last_stored")
        block = ctx.enter_context(nc.Block())

        @block.gpsimd
        def _(pool):
            nc.gpsimd.memset(norm.power[:], -0.5).then_inc(norm.power_ready, 1)
            pool.wait_ge(norm.power_ready, 1)
            pipeline(pool, NT, [(0, lambda t, j, r: norm.gpsimd(pool, t, j))])

        @block.vector
        def _(dve):
            def normalise(t, j, r):
                norm.vector(dve, t, j, quantised=first)

            def make_hidden(t, j, r):
                dve.wait_ge(gated, t + 1)
                nc.vector.tensor_tensor(gate[:, j, :], gate[:, j, :], gate_ps[:, 0:FF], ALU.mult).then_inc(sized, 1)
                dve.wait_ge(sized, t + 1)
                nc.vector.tensor_tensor(hidden[:, j, :], gate[:, j, :], up_ps[:, 0:FF], ALU.mult).then_inc(hiddens, 1)
                dve.wait_ge(hiddens, t + 1)
                after(dve, turns, t - 1)
                second.vector(dve, t, hidden[:, j, :], level[:, j, :])

            def add_result(t, j, r):
                for half in range(2):
                    dve.wait_ge(results, 2 * t + half + 1)
                    tile = c.x[:, bass.ds(t, 1), half * HALF:(half + 1) * HALF]
                    nc.vector.tensor_tensor(tile, tile, result_ps[:, half:half + 1, :], ALU.add).then_inc(summed, 1)

            pipeline(dve, NT, [(1, normalise), (0, make_hidden), (0, add_result)])

        @block.scalar
        def _(act):
            def plain_sign(t, j, r):
                act.wait_ge(norm.plain_ready, t + 1)
                first.scalar(act, t, norm.normal[:, j, :])

            def squash(t, j, r):
                act.wait_ge(norm.products, t + 1)
                after(act, second.done, t - 1)
                nc.scalar.activation(gate[:, j, :], gate_ps[:, 0:FF], ACT.Sigmoid).then_inc(gated, 1)

            def hidden_sign(t, j, r):
                act.wait_ge(hiddens, t + 1)
                second.scalar(act, t, hidden[:, j, :])

            def take(t, j, r):
                act.wait_ge(turns, t + 1)
                after(act, results, 2 * (t - 1))
                for b in range(FB):
                    rows = min(P, FF - b * P)
                    ins = nc.scalar.copy(hidden_turned[0:rows, j, b, :], hidden_ps[0:rows, b * P:(b + 1) * P])
                ins.then_inc(taken, 1)

            pipeline(act, NT, [(1, plain_sign), (1, lambda t, j, r: norm.scalar(act, t, j)), (0, squash),
                               (0, hidden_sign), (0, take)])

        @block.tensor
        def _(pe):
            def multiply(t, j, r):
                pe.wait_ge(norm.taken, 2 * t + 2)
                after(pe, hiddens, t)
                for side, bank in ((0, gate_ps), (1, up_ps)):
                    for k in range(KT):
                        ins = pe.matmul(bank[:, 0:FF], norm.turned_sb[:, j, k, :], in_turned[:, k, side * FF:(side + 1) * FF],
                                        start=(k == 0), stop=(k == KT - 1))
                ins.then_inc(norm.products, 1)

            def turn_hidden(t, j, r):
                pe.wait_ge(second.done, t + 1)
                after(pe, taken, t)
                for b in range(FB):
                    cols = min(P, FF - b * P)
                    ins = pe.transpose(hidden_ps[0:cols, b * P:(b + 1) * P], level[:, j, b * P:b * P + cols], c.ident[:])
                ins.then_inc(turns, 1)

            def project(t, j, r):
                pe.wait_ge(taken, t + 1)
                for half in range(2):
                    after(pe, summed, 2 * (t - 1) + half + 1)
                    for b in range(FB):
                        rows = min(P, FF - b * P)
                        ins = pe.matmul(result_ps[:, half, :], hidden_turned[0:rows, j, b, :],
                                        down_turned[0:rows, b, half * HALF:(half + 1) * HALF], start=(b == 0), stop=(b == FB - 1))
                    ins.then_inc(results, 1)

            pipeline(pe, NT, [(1, lambda t, j, r: norm.tensor(pe, t, j)), (0, multiply), (0, turn_hidden), (0, project)])

        @block.sync
        def _(sp):
            for t in range(NT):
                rows = P if t < NT - 1 else LAST
                sp.wait_ge(summed, 2 * t + 2)
                sp.dma_start(out[t * P:t * P + rows, :], c.x[0:rows, t, :]).then_inc(stored, 16)
            sp.wait_ge(stored, 16 * NT)


def gnn_ffn_kernel(nc, x, src, dst, edge_weight, gnn_bias, router_w, router_b, w1, b1, w2, b2,
                   rms_w, w_down, w_l, w_r, att, w_up, q_gate, q_up, q_down, out):
    edge_rows = nc.dram_tensor("edge_rows", [P * NS, 4], F32, kind="Internal").ap()
    token_rows = nc.dram_tensor("token_rows", [XS * P, D], F32, kind="Internal").ap()
    expert_rows = nc.dram_tensor("expert_rows", [XS * P, D], F32, kind="Internal").ap()
    left_rows = nc.dram_tensor("left_rows", [NT * P, HD], F32, kind="Internal").ap()
    with ExitStack() as ctx:
        sb, ps, sem = pools(nc, ctx)
        c = Shared()
        c.x = sb("x_nodes", [P, NT, D])
        c.iota = sb("iota", [P, D], F16)
        c.part = sb("part", [P, 1])
        c.ones = sb("ones", [P, P])
        c.before = sb("before", [P, P])
        c.ident = sb("ident", [P, P])
        c.big_ident = sb("big_ident", [P, NH, P], BF16)
        c.row_select = sb("row_select", [3 * GH, GH, P], BF16)
        c.ident_b = sb("ident_b", [P, P], BF16)
        c.edges = sb("edges", [P, NS, 4])
        c.source_i = sb("source_i", [P, NS], I32)
        c.group_tile = sb("group_tile", [1, NG], I32)
        c.token_place = sb("token_place", [P, NT], I32)
        c.slot_expert = sb("slot_expert", [1, XS], I32)
        c.unit_number = c.iota
        build_constants(nc, c, edge_rows, token_rows, x)
        sort_edges(nc, c, src, dst, edge_weight, edge_rows)
        with ExitStack() as inner:
            mix = pools(nc, inner)[0]("mix", [P, NT, D])
            build_weights(nc, c, mix)
            apply_mix(nc, c, mix, gnn_bias)
        route(nc, c, router_w, router_b, token_rows)
        run_experts(nc, c, w1, b1, w2, b2, token_rows, expert_rows)
        with ExitStack() as inner:
            sbi = pools(nc, inner)[0]
            both = sbi("left_right", [P, NT, 2 * HD])
            right_parts = sbi("right_parts", [P, NT, 3 * HD], BF16)
            best = sbi("best_score", [P, NT, NH])
            total = sbi("weighted_total", [P, NT, NH, HW1])
            c.att_rows = sbi("att_rows", [P, HD])
            attention_inputs(nc, c, att, w_down, w_l, w_r, rms_w, expert_rows, left_rows, both, right_parts, best, total)
            attend(nc, c, left_rows, both, right_parts, best, total)
            attention_output(nc, c, w_up, total)
        quantised_feed_forward(nc, c, q_gate, q_up, q_down, out)


INPUTS = ["x", "src", "dst", "edge_weight", "L0_gnn_bias", "L0_ffn_router_w", "L0_ffn_router_b", "L0_ffn_w1",
          "L0_ffn_b1", "L0_ffn_w2", "L0_ffn_b2", "L1_gnn_rms_w", "L1_gnn_W_down", "L1_gnn_Wl", "L1_gnn_Wr",
          "L1_gnn_att", "L1_gnn_W_up", "L1_ffn_w_gate", "L1_ffn_w_up", "L1_ffn_w_down"]


def kernel(**inputs):
    import numpy as np
    import concourse.bacc as bacc
    from concourse.bass_utils import run_bass_kernel_spmd

    nc = bacc.Bacc("TRN2", target_bir_lowering=False, num_devices=1)
    arrays, args = {}, []
    for name in INPUTS:
        a = np.ascontiguousarray(inputs[name])
        arrays["in_" + name] = a
        args.append(nc.dram_tensor("in_" + name, a.shape, mybir.dt.from_np(a.dtype), kind="ExternalInput").ap())
    out = nc.dram_tensor("out", (N, D), F32, kind="ExternalOutput").ap()
    gnn_ffn_kernel(nc, *args, out)
    result = run_bass_kernel_spmd(nc, [arrays], core_ids=[0])
    return result.results[0]["out"]
```
